# Optimizing a Trainium2 kernel written in Bass

```python
import numpy as np
import jax
import jax.numpy as jnp

def _softmax(x, axis=-1):
    return jax.nn.softmax(x, axis=axis)

def _gelu(x):
    return jax.nn.gelu(x, approximate=True)

def _silu(x):
    return jax.nn.silu(x)

def _sigmoid(x):
    return jax.nn.sigmoid(x)

def _layernorm(x, axis=-1, eps=1e-05):
    m = jnp.mean(x, axis=axis, keepdims=True)
    v = jnp.var(x, axis=axis, keepdims=True)
    return (x - m) / jnp.sqrt(v + eps)

def _scatter_add(tgt, idx, src, axis=0):
    return tgt.at[idx].add(src)

def _segment_sum(src, seg, n):
    return jax.ops.segment_sum(src, seg, n)
kernel_name = 'mk_adj_resnorm_d2_adj_r2_3d3980'

def setup_inputs(seed: int=0):
    np.random.seed(seed)
    _w = jnp.asarray

    def _rec_inputs():
        import jax
        import jax.numpy as jnp
        _gk = jax.random.key(seed)
        x = -0.0005207 + 1.001 * jax.random.normal(jax.random.fold_in(_gk, 1), (64, 128, 128), jnp.float32)
        _a = jax.random.bernoulli(jax.random.fold_in(_gk, 2), 0.015625, (128, 128))
        _a = jnp.logical_or(_a, jnp.eye(128, dtype=bool))
        _af = _a.astype(jnp.float32)
        adj = _af
        return (x, adj)
    x, adj = _rec_inputs()

    def _L0_gnn_setup():
        import jax, jax.numpy as jnp
        import numpy as np
        B, N, IN_DIM, OUT_DIM, H = (2, 2048, 128, 128, 4)
        HEAD_DIM = OUT_DIM // H
        EDGE_P = 0.01
        key = jax.random.key(seed)
        k1, k2, k3 = jax.random.split(key, 3)
        h = jax.random.normal(k1, (B, N, IN_DIM), dtype=jnp.float32)
        W = jax.random.normal(k2, (IN_DIM, 3 * OUT_DIM), dtype=jnp.float32) / np.sqrt(IN_DIM)
        adj = (jax.random.uniform(k3, (N, N)) < EDGE_P).astype(jnp.float32)
        adj = jnp.maximum(adj, jnp.eye(N, dtype=jnp.float32))
        return {'h': h, 'W': W, 'adj': adj}
    _L0_gnn_all = _L0_gnn_setup()
    _L0_gnn_in = {k: v for k, v in _L0_gnn_all.items() if k in ('W',)}
    del _L0_gnn_all

    def _L1_gnn_setup():
        import jax, jax.numpy as jnp
        import numpy as np
        B, T, D, H = (64, 1024, 128, 128)
        MAX_SKIP = 4

        def _lstm_last(Wih, Whh, bih, bhh, xs):
            N, _, Hd = xs.shape
            bias = bih + bhh

            def step(carry, x_t):
                h, c = carry
                g = x_t @ Wih.T + h @ Whh.T + bias
                i, f, gg, o = jnp.split(g, 4, axis=-1)
                c = jax.nn.sigmoid(f) * c + jax.nn.sigmoid(i) * jnp.tanh(gg)
                h = jax.nn.sigmoid(o) * jnp.tanh(c)
                return ((h, c), None)
            init = (jnp.zeros((N, Hd), xs.dtype), jnp.zeros((N, Hd), xs.dtype))
            (h_last, _), _ = jax.lax.scan(step, init, jnp.swapaxes(xs, 0, 1))
            return h_last
        key = jax.random.key(seed)
        ks = jax.random.split(key, 8)
        s = 0.05
        x = jax.random.normal(ks[0], (B, T, D), jnp.float32)
        adj = jax.random.uniform(ks[1], (T, T), jnp.float32) / T
        Wg0 = jax.random.normal(ks[2], (D, H), jnp.float32) * s
        bg0 = jnp.zeros((H,), jnp.float32)
        Wg1 = jax.random.normal(ks[3], (H, H), jnp.float32) * s
        bg1 = jnp.zeros((H,), jnp.float32)
        Wih = jax.random.normal(ks[4], (MAX_SKIP, 4 * H, H), jnp.float32) * s
        Whh = jax.random.normal(ks[5], (MAX_SKIP, 4 * H, H), jnp.float32) * s
        bih = jax.random.normal(ks[6], (MAX_SKIP, 4 * H), jnp.float32) * s
        bhh = jax.random.normal(ks[7], (MAX_SKIP, 4 * H), jnp.float32) * s
        return dict(x=x, adj=adj, Wg0=Wg0, bg0=bg0, Wg1=Wg1, bg1=bg1, Wih=Wih, Whh=Whh, bih=bih, bhh=bhh)
    _L1_gnn_all = _L1_gnn_setup()
    _L1_gnn_in = {k: v for k, v in _L1_gnn_all.items() if k in ('Wg0', 'bg0', 'Wg1', 'bg1', 'Wih', 'Whh', 'bih', 'bhh')}
    del _L1_gnn_all
    return {'x': x, 'adj': adj, 'L0_gnn_W': _L0_gnn_in['W'], 'L1_gnn_Wg0': _L1_gnn_in['Wg0'], 'L1_gnn_bg0': _L1_gnn_in['bg0'], 'L1_gnn_Wg1': _L1_gnn_in['Wg1'], 'L1_gnn_bg1': _L1_gnn_in['bg1'], 'L1_gnn_Wih': _L1_gnn_in['Wih'], 'L1_gnn_Whh': _L1_gnn_in['Whh'], 'L1_gnn_bih': _L1_gnn_in['bih'], 'L1_gnn_bhh': _L1_gnn_in['bhh']}

def reference(x, adj, L0_gnn_W, L1_gnn_Wg0, L1_gnn_bg0, L1_gnn_Wg1, L1_gnn_bg1, L1_gnn_Wih, L1_gnn_Whh, L1_gnn_bih, L1_gnn_bhh):
    import jax
    import jax.numpy as jnp

    def _L0_gnn_ref(h, W, adj):
        import jax, jax.numpy as jnp
        import numpy as np
        B, N, IN_DIM, OUT_DIM, H = (2, 2048, 128, 128, 4)
        HEAD_DIM = OUT_DIM // H
        EDGE_P = 0.01
        Bn, Nn, _ = h.shape
        qkv = h @ W
        qkv = qkv.reshape(Bn, Nn, 3, H, HEAD_DIM).transpose(2, 0, 3, 1, 4)
        q, k, v = (qkv[0], qkv[1], qkv[2])
        mask = jnp.where(adj == 0, -jnp.inf, 0.0)
        scores = jnp.einsum('bhid,bhjd->bhij', q, k) / np.sqrt(HEAD_DIM) + mask
        attn = jax.nn.softmax(scores, axis=-1)
        out = jnp.einsum('bhij,bhjd->bhid', attn, v)
        return out.transpose(0, 2, 1, 3).reshape(Bn, Nn, OUT_DIM)

    def _L1_gnn_ref(x, adj, Wg0, bg0, Wg1, bg1, Wih, Whh, bih, bhh):
        import jax, jax.numpy as jnp
        import numpy as np
        B, T, D, H = (64, 1024, 128, 128)
        MAX_SKIP = 4

        def _lstm_last(Wih, Whh, bih, bhh, xs):
            N, _, Hd = xs.shape
            bias = bih + bhh

            def step(carry, x_t):
                h, c = carry
                g = x_t @ Wih.T + h @ Whh.T + bias
                i, f, gg, o = jnp.split(g, 4, axis=-1)
                c = jax.nn.sigmoid(f) * c + jax.nn.sigmoid(i) * jnp.tanh(gg)
                h = jax.nn.sigmoid(o) * jnp.tanh(c)
                return ((h, c), None)
            init = (jnp.zeros((N, Hd), xs.dtype), jnp.zeros((N, Hd), xs.dtype))
            (h_last, _), _ = jax.lax.scan(step, init, jnp.swapaxes(xs, 0, 1))
            return h_last
        h = jax.nn.relu(jnp.einsum('ts,bsh->bth', adj, x @ Wg0 + bg0))
        h = jax.nn.relu(jnp.einsum('ts,bsh->bth', adj, h @ Wg1 + bg1))
        Bv, Tv, Hd = h.shape
        for p in range(1, MAX_SKIP + 1):
            nw = Tv // p
            wins = h[:, :nw * p, :].reshape(Bv * nw, p, Hd)
            last = _lstm_last(Wih[p - 1], Whh[p - 1], bih[p - 1], bhh[p - 1], wins)
            idx = jnp.arange(nw) * p + (p - 1)
            h = h.at[:, idx, :].set(last.reshape(Bv, nw, Hd))
        return h
    x = _layernorm(x + _L0_gnn_ref(x, L0_gnn_W, adj), axis=-1)
    x = _layernorm(x + _L1_gnn_ref(x, adj, L1_gnn_Wg0, L1_gnn_bg0, L1_gnn_Wg1, L1_gnn_bg1, L1_gnn_Wih, L1_gnn_Whh, L1_gnn_bih, L1_gnn_bhh), axis=-1)
    return x

_drawn_inputs = setup_inputs


def setup_inputs(seed=0):
    import zlib

    import numpy as np

    out = dict(_drawn_inputs(seed))
    spreads = {'L1_gnn_bg0': (0.0, 0.58), 'L1_gnn_bg1': (0.0, 0.573)}
    factors = {'L1_gnn_Whh': 8.0, 'L1_gnn_bih': 2.875, 'L1_gnn_bhh': 2.926}
    for name, (base, spread) in spreads.items():
        noise = np.random.default_rng([zlib.crc32(name.encode()), seed]).standard_normal(out[name].shape)
        drawn = base * np.exp(spread * noise) if base else spread * noise
        out[name] = jnp.asarray(drawn.astype(out[name].dtype))
    for name, factor in factors.items():
        out[name] = (out[name] * factor).astype(out[name].dtype)
    return out
```

```python
from contextlib import ExitStack

import concourse.bass as bass
from concourse import mybir

F32 = mybir.dt.float32
F32R = mybir.dt.float32r
BF16 = mybir.dt.bfloat16
ALU = mybir.AluOpType
ACT = mybir.ActivationFunctionType
AX = mybir.AxisListType

D = 128
HEADS = 4
HD = D // HEADS
GB = 4
GW = GB * D
EPS = 1e-5
MASKED = -1e30
ATTN_LAG = 4
UNROLL = 4

UB = 8
UW = UB * D
MAX_SKIP = 4
GATE_I, GATE_F, GATE_G, GATE_O = range(4)


def need(eng, sem, n):
    if isinstance(n, int) and n <= 0:
        return
    eng.wait_ge(sem, n)


def lstm_slots():
    slots = [(1, 0, 0), (1, 0, 1)]
    for p in range(2, MAX_SKIP + 1):
        slots += [(p, s, None) for s in range(p)]
    return slots


def slot_gates(step):
    return [GATE_I, GATE_G, GATE_O] if step == 0 else [GATE_I, GATE_G, GATE_F, GATE_O]


def adjacent_residual_kernel(nc, x_cols, x_rows, adj, adj_t, w_qkv, w_g0, b_g0, w_g1, b_g1,
                             w_ih, w_hh, b_ih, b_hh, eye, out):
    n_cols = x_cols.shape[1]
    groups = n_cols // GW
    units = n_cols // UW
    slots = lstm_slots()

    with ExitStack() as top:
        def sb(name, shape, dt=F32, ctx=top):
            return ctx.enter_context(nc.sbuf_tensor(name, shape, dt))

        def sem(name):
            return top.enter_context(nc.semaphore(name))

        psum = top.enter_context(nc.psum_tensor("psum", [D, 8, GW], F32))

        h2_cols = sb("h2_cols", [D, n_cols])
        x1_rows = sb("x1_rows", [D, n_cols])
        ident = sb("ident", [D, D])
        w_in1 = sb("w_in1", [D, 4 * D])
        w_hi = sb("w_hi", [D, 3, 2, 4 * D], F32R)
        w_lo = sb("w_lo", [D, 3, 2, 4 * D], F32R)
        tick = sb("tick", [D, 2])
        tock = sb("tock", [D, 2])
        eps = sb("eps", [D, 2 * GB])
        minus_half = sb("minus_half", [D, 2 * GB])
        b_lstm = sb("b_lstm", [D, MAX_SKIP, 4])

        with ExitStack() as ctx:
            def s1(name, shape, dt=F32):
                return sb(name, shape, dt, ctx)

            xt = s1("xt", [D, 2, GW])
            xr = s1("xr", [D, 2, GW])
            wq = s1("wq", [D, 3 * D])
            wg0 = s1("wg0", [D, D])
            wg1 = s1("wg1", [D, D])
            adj_sb = s1("adj_sb", [D, D])
            adjt_sb = s1("adjt_sb", [D, D])
            bg0 = s1("bg0", [D, D])
            bg1 = s1("bg1", [D, 1])
            b_raw = s1("b_raw", [D, 2, MAX_SKIP, 4])
            w_raw = s1("w_raw", [D, 2, 4 * D])
            ident_bf = s1("ident_bf", [D, D], BF16)
            mask_bf = s1("mask_bf", [D, HEADS, D], BF16)
            ones = s1("ones", [D, D])
            deg_col = s1("deg_col", [D, 1])
            bias0 = s1("bias0", [D, D])
            bias1 = s1("bias1", [D, D])
            q_sb = s1("q_sb", [D, 2, GW])
            k_sb = s1("k_sb", [D, 2, HEADS, GW])
            v_sb = s1("v_sb", [D, 4, GW])
            sc = s1("sc", [D, 2, GW])
            mx = s1("mx", [D, 2, HEADS])
            pr = s1("pr", [D, 2, GB, GW])
            den = s1("den", [D, 4, GB * HEADS])
            rden = s1("rden", [D, GB * HEADS])
            pt = s1("pt", [D, 2, GW])
            ot = s1("ot", [D, 2, GW])
            att = s1("att", [D, 2, GW])
            res = s1("res", [D, 2, GW])
            st6 = s1("st6", [D, GB, 6])
            mv = s1("mv", [D, 2, GB, 2])
            veps = s1("veps", [D, 2, GB])
            rstd = s1("rstd", [D, 2, GB])
            x1 = s1("x1", [D, 2, GW])
            y1 = s1("y1", [D, 2, GW])
            h1a = s1("h1a", [D, 2, GW])
            h1 = s1("h1", [D, 2, GW])
            y2 = s1("y2", [D, 2, GW])
            h2a = s1("h2a", [D, 2, GW])

            consts_in = sem("consts_in")
            xt_in = [sem("xt_in0"), sem("xt_in1")]
            xr_in = [sem("xr_in0"), sem("xr_in1")]
            w_in = [sem("w_in0"), sem("w_in1s")]
            w1_in = sem("w1_in")
            x1_kept = [sem("x1_kept0"), sem("x1_kept1")]
            k_zeroed = sem("k_zeroed")
            setup_dve = sem("setup_dve")
            mask_ready = sem("mask_ready")
            bias1_ready = sem("bias1_ready")
            ones_ready = sem("ones_ready")
            degree_mm = sem("degree_mm")
            w_hi_done, w_split = sem("w_hi_done"), sem("w_split")
            q_mm, k_mm, v_mm = sem("q_mm"), sem("k_mm"), sem("v_mm")
            q_ready, k_ready, v_ready = sem("q_ready"), sem("k_ready"), sem("v_ready")
            score_mm, max_ready, shifted, exp_ready = sem("score_mm"), sem("max_ready"), sem("shifted"), sem("exp_ready")
            den_ready = sem("den_ready")
            pt_mm, pt_ready, pv_mm, ot_ready, ot_rows = sem("pt_mm"), sem("pt_ready"), sem("pv_mm"), sem("ot_ready"), sem("ot_rows")
            rden_ready, att_ready, res_ready, stats_ready, moments_ready = (
                sem("rden_ready"), sem("att_ready"), sem("res_ready"), sem("stats_ready"), sem("moments_ready"))
            half_set, veps_ready = sem("half_set"), sem("veps_ready")
            rstd_ready, x1_ready = sem("rstd_ready"), sem("x1_ready")
            y1_mm, y1_ready, h1_mm, h1_added, h1_ready = (
                sem("y1_mm"), sem("y1_ready"), sem("h1_mm"), sem("h1_added"), sem("h1_ready"))
            y2_mm, y2_ready, h2_mm, h2_added, h2_ready = (
                sem("y2_mm"), sem("y2_ready"), sem("h2_mm"), sem("h2_added"), sem("h2_ready"))

            def holds(it, lag):
                return not isinstance(it, int) or 0 <= it - lag < groups

            def iterations(eng, body):
                begin = ATTN_LAG + 1
                turns = (groups - begin) // UNROLL
                for it in range(begin):
                    body(it, it % UNROLL)
                with eng.Fori(0, turns) as turn:
                    for it in range(begin, begin + UNROLL):
                        body(turn * UNROLL + it, it % UNROLL)
                for it in range(begin + turns * UNROLL, groups + ATTN_LAG):
                    body(it, it % UNROLL)

            def slot_dmas(it, j, lag):
                return (it - j) * 8 + 16 * ((j - lag) // 2)

            def cols(g, width=GW):
                return bass.ds(g * width, width)

            with nc.Block() as block:
                @block.sync
                def _(sp):
                    def body(it, j):
                        fixed = isinstance(it, int)
                        used = it - 1 if fixed else sp.snap(it - 1)
                        passed = it - 3 if fixed else sp.snap(it - 3)
                        at, at2 = ((it - lag) * GW if fixed else sp.snap((it - lag) * GW) for lag in (0, 2))
                        if holds(it, 0):
                            need(sp, v_mm, used)
                            sp.dma_start(xt[:, j % 2], x_cols[:, bass.ds(at, GW)]).then_inc(xt_in[j % 2], 16)
                        if isinstance(it, int) and it == 0:
                            for dst, src in ((adj_sb[:], adj), (adjt_sb[:], adj_t), (ident[:], eye), (wg0[:], w_g0), (wg1[:], w_g1),
                                             (bg0[:], b_g0), (bg1[:], b_g1), (b_raw[:, 0], b_ih), (b_raw[:, 1], b_hh)):
                                sp.dma_start(dst, src).then_inc(consts_in, 16)
                        if isinstance(it, int) and it == 1:
                            sp.dma_start(w_in1[:], w_ih[:, 0]).then_inc(w1_in, 16)
                            for n in range(6):
                                need(sp, w_split, n - 1)
                                src = (w_ih if n % 2 == 0 else w_hh)[:, 1 + n // 2]
                                sp.dma_start(w_raw[:, n % 2], src).then_inc(w_in[n % 2], 16)
                        if holds(it, 2):
                            need(sp, res_ready, passed)
                            sp.dma_start(xr[:, j % 2], x_rows[:, bass.ds(at2, GW)]).then_inc(xr_in[j % 2], 16)

                    sp.dma_start(wq[:], w_qkv).then_inc(consts_in, 16)
                    iterations(sp, body)
                    for s in x1_kept:
                        sp.wait_ge(s, 16 * (groups // 2))

                N_CONSTS = 10

                @block.tensor
                def _(pe):
                    def transposes_of_p(it, j, b):
                        n = (it - 2) * GB + b
                        pe.wait_ge(exp_ready, n + 1)
                        need(pe, pt_ready, n - 1)
                        for h in range(HEADS):
                            mm = nc.tensor.transpose(psum[:, 5 + b % 2, h * D:(h + 1) * D],
                                                     pr[:, j % 2, b, h * D:(h + 1) * D], ident[:])
                        mm.then_inc(pt_mm, 1)

                    def probs_times_v(it, j, b):
                        g = it - 2
                        n = g * GB + b
                        pe.wait_ge(pt_ready, n + 1)
                        if b == 0:
                            pe.wait_ge(v_ready, g + 1)
                            need(pe, *((ot_ready, g) if holds(it, 3) else (bias1_ready, 1)))
                        for h in range(HEADS):
                            mm = nc.tensor.matmul(psum[HD * h:HD * h + HD, 7, b * D:(b + 1) * D],
                                                  v_sb[:, (j + 2) % 4, b * D + HD * h:b * D + HD * h + HD],
                                                  pt[:, b % 2, h * D:(h + 1) * D], start=True, stop=True)
                        mm.then_inc(pv_mm, 1)

                    def scores(it, j, b):
                        g = it - 1
                        n = g * GB + b
                        bank = psum[:, 3 + b % 2, :]
                        if b == 0:
                            pe.wait_ge(q_ready, g + 1)
                            pe.wait_ge(k_ready, g + 1)
                        need(pe, shifted, n - 1)
                        nc.tensor.matmul(bank, ident_bf[:], mask_bf[:].rearrange("p h k -> p (h k)"),
                                         start=True, stop=False)
                        nc.tensor.matmul(bank, q_sb[:, (j + 1) % 2, b * D:(b + 1) * D],
                                         k_sb[:, (j + 1) % 2, :, b * D:(b + 1) * D],
                                         start=False, stop=True).then_inc(score_mm, 1)

                    def body(it, j):
                        first, drained = isinstance(it, int) and it == 0, not holds(it, 0)
                        if holds(it, 0):
                            pe.wait_ge(xt_in[j % 2], slot_dmas(it, j, 0) + 16)
                            need(pe, *((y1_ready, it - 3) if holds(it, 4) else (q_ready, it)))
                            nc.tensor.matmul(psum[:, 0, :], wq[:, 0:D], xt[:, j % 2, :],
                                             start=True, stop=True).then_inc(q_mm, 1)
                            need(pe, *((h1_added, it - 3) if holds(it, 4) else (k_ready, it)))
                            nc.tensor.matmul(psum[:, 1, :], wq[:, D:2 * D], xt[:, j % 2, :],
                                             start=True, stop=True).then_inc(k_mm, 1)
                            need(pe, *((h2_added, it - 4) if holds(it, 5) else (v_ready, it)))
                            for b in range(GB):
                                mm = nc.tensor.matmul(psum[:, 2, b * D:(b + 1) * D], xt[:, j % 2, b * D:(b + 1) * D],
                                                      wq[:, 2 * D:3 * D], start=True, stop=True)
                            mm.then_inc(v_mm, 1)
                        if first:
                            pe.wait_ge(ones_ready, 1)
                            nc.tensor.matmul(psum[:, 7, 0:D], ones[:], adjt_sb[:], start=True, stop=True).then_inc(degree_mm, 1)
                        if holds(it, 3):
                            g = it - 3
                            pe.wait_ge(ot_ready, g + 1)
                            if drained:
                                need(pe, y1_ready, it - 3)
                            else:
                                pe.wait_ge(q_ready, it + 1)
                            for b in range(GB):
                                mm = nc.tensor.transpose(psum[:, 0, b * D:(b + 1) * D],
                                                         ot[:, (j + 1) % 2, b * D:(b + 1) * D], ident[:])
                            mm.then_inc(ot_rows, 1)
                        if holds(it, 1):
                            if isinstance(it, int) and it == 1:
                                pe.wait_ge(mask_ready, 2)
                            scores(it, j, 0)
                            scores(it, j, 1)
                        if holds(it, 4):
                            g = it - 4
                            pe.wait_ge(h1_ready, g + 1)
                            if not drained:
                                pe.wait_ge(k_ready, it + 1)
                            for b in range(GB):
                                mm = nc.tensor.matmul(psum[:, 1, b * D:(b + 1) * D], h1[:, j % 2, b * D:(b + 1) * D],
                                                      adjt_sb[:], start=True, stop=True)
                            mm.then_inc(y2_mm, 1)
                        if holds(it, 1):
                            scores(it, j, 2)
                            scores(it, j, 3)
                        if holds(it, 4):
                            g = it - 4
                            pe.wait_ge(y2_ready, g + 1)
                            if drained:
                                need(pe, h2_added, g)
                            else:
                                pe.wait_ge(v_ready, it + 1)
                            nc.tensor.matmul(psum[:, 2, :], wg1[:], y2[:, j % 2, :], start=True, stop=True).then_inc(h2_mm, 1)
                        if holds(it, 2):
                            transposes_of_p(it, j, 0)
                            transposes_of_p(it, j, 1)
                            probs_times_v(it, j, 0)
                        if holds(it, 3):
                            g = it - 3
                            pe.wait_ge(x1_ready, g + 1)
                            pe.wait_ge(att_ready, g + 1)
                            for b in range(GB):
                                mm = nc.tensor.matmul(psum[:, 0, b * D:(b + 1) * D], x1[:, (j + 1) % 2, b * D:(b + 1) * D],
                                                      adjt_sb[:], start=True, stop=True)
                            mm.then_inc(y1_mm, 1)
                        if holds(it, 2):
                            transposes_of_p(it, j, 2)
                            probs_times_v(it, j, 1)
                            transposes_of_p(it, j, 3)
                            probs_times_v(it, j, 2)
                            probs_times_v(it, j, 3)
                        if holds(it, 3):
                            g = it - 3
                            pe.wait_ge(y1_ready, g + 1)
                            if holds(it, 4):
                                pe.wait_ge(y2_ready, it - 3)
                            elif not drained:
                                pe.wait_ge(k_ready, it + 1)
                            for b in range(GB):
                                mm = nc.tensor.matmul(psum[:, 1, b * D:(b + 1) * D], y1[:, (j + 1) % 2, b * D:(b + 1) * D],
                                                      wg0[:], start=True, stop=True)
                            mm.then_inc(h1_mm, 1)

                    pe.wait_ge(consts_in, 16 * N_CONSTS)
                    iterations(pe, body)

                @block.scalar
                def _(act):
                    def exps(it, j, b):
                        n = (it - 1) * GB + b
                        act.wait_ge(shifted, n + 1)
                        need(act, pt_mm, n - 7)
                        need(act, den_ready, n - 7)
                        nc.scalar.activation(pr[:, (j + 1) % 2, b, :], sc[:, b % 2, :], ACT.Exp).then_inc(exp_ready, 1)

                    def copies_of_pt(it, b):
                        n = (it - 2) * GB + b
                        act.wait_ge(pt_mm, n + 1)
                        need(act, pv_mm, n - 1)
                        nc.scalar.activation(pt[:, b % 2, :], psum[:, 5 + b % 2, :], ACT.Copy).then_inc(pt_ready, 1)

                    def body(it, j):
                        if holds(it, 0):
                            need(act, score_mm, (it - 1) * GB)
                            act.wait_ge(q_mm, it + 1)
                            nc.scalar.activation(q_sb[:, j % 2, :], psum[:, 0, :], ACT.Copy,
                                                 scale=float(HD) ** -0.5).then_inc(q_ready, 1)
                            act.wait_ge(k_mm, it + 1)
                            for h in range(HEADS):
                                ins = nc.scalar.activation(k_sb[HD * h:HD * h + HD, j % 2, h, :],
                                                           psum[HD * h:HD * h + HD, 1, :], ACT.Copy)
                            ins.then_inc(k_ready, 1)
                        if holds(it, 1):
                            exps(it, j, 0)
                            exps(it, j, 1)
                        if holds(it, 4):
                            act.wait_ge(y2_mm, it - 3)
                            nc.scalar.activation(y2[:, j % 2, :], psum[:, 1, :], ACT.Copy).then_inc(y2_ready, 1)
                        if holds(it, 1):
                            exps(it, j, 2)
                        if holds(it, 2):
                            copies_of_pt(it, 0)
                            copies_of_pt(it, 1)
                        if holds(it, 1):
                            exps(it, j, 3)
                        if holds(it, 3):
                            act.wait_ge(y1_mm, it - 2)
                            need(act, h1_mm, it - 4)
                            nc.scalar.activation(y1[:, (j + 1) % 2, :], psum[:, 0, :], ACT.Copy).then_inc(y1_ready, 1)
                        if holds(it, 2):
                            copies_of_pt(it, 2)
                            copies_of_pt(it, 3)
                            act.wait_ge(pv_mm, (it - 1) * GB)
                            need(act, ot_rows, it - 3)
                            nc.scalar.activation(ot[:, j % 2, :], psum[:, 7, :], ACT.Copy).then_inc(ot_ready, 1)
                        if holds(it, 4):
                            act.wait_ge(x1_ready, it - 3)
                            act.dma_start(x1_rows[:, cols(it - 4)], x1[:, j % 2]).then_inc(x1_kept[j % 2], 16)
                        if holds(it, 3):
                            act.wait_ge(h1_added, it - 2)
                            need(act, y2_mm, it - 4)
                            nc.scalar.activation(h1[:, (j + 1) % 2, :], h1a[:, (j + 1) % 2, :], ACT.Relu).then_inc(h1_ready, 1)
                        if holds(it, 4):
                            act.wait_ge(h2_added, it - 3)
                            nc.scalar.activation(h2_cols[:, cols(it - 4)], h2a[:, j % 2, :], ACT.Relu).then_inc(h2_ready, 1)

                    act.wait_ge(k_zeroed, 1)
                    iterations(act, body)

                @block.vector
                def _(dve):
                    dve.wait_ge(consts_in, 16 * N_CONSTS)
                    nc.vector.memset(ones[:], 1.0).then_inc(ones_ready, 1)
                    nc.vector.memset(tick[:], 0.0).then_inc(setup_dve, 1)
                    nc.vector.tensor_copy(ident_bf[:], ident[:]).then_inc(mask_ready, 1)
                    for h in range(HEADS):
                        ins = nc.vector.tensor_scalar(mask_bf[:, h, :], adj_sb[:], 0.0, MASKED, ALU.is_equal, ALU.mult)
                    ins.then_inc(mask_ready, 1)
                    nc.vector.tensor_reduce(deg_col[:], adj_sb[:], AX.X, ALU.add).then_inc(setup_dve, 1)
                    nc.vector.tensor_tensor(b_lstm[:], b_raw[:, 0], b_raw[:, 1], ALU.add)
                    dve.wait_ge(setup_dve, 2)
                    nc.vector.tensor_scalar(bias0[:], bg0[:], deg_col[:, 0:1], None, ALU.mult).then_inc(setup_dve, 1)
                    dve.wait_ge(degree_mm, 1)
                    nc.vector.tensor_scalar(bias1[:], psum[:, 7, 0:D], bg1[:, 0:1], None, ALU.mult).then_inc(bias1_ready, 1)
                    dve.wait_ge(setup_dve, 3)
                    dve.wait_ge(bias1_ready, 1)

                    def max_of(it, j, b):
                        n = (it - 1) * GB + b
                        dve.wait_ge(score_mm, n + 1)
                        nc.vector.tensor_reduce(mx[:, b % 2, :], psum[:, 3 + b % 2, :].rearrange("p (h k) -> p h k", h=HEADS),
                                                AX.X, ALU.max).then_inc(max_ready, 1)

                    def shift(it, j, b):
                        n = (it - 1) * GB + b
                        dve.wait_ge(max_ready, n + 1)
                        need(dve, exp_ready, n - 1)
                        nc.vector.tensor_tensor(sc[:, b % 2, :].rearrange("p (h k) -> p h k", h=HEADS),
                                                psum[:, 3 + b % 2, :].rearrange("p (h k) -> p h k", h=HEADS),
                                                mx[:, b % 2, :].unsqueeze(2).to_broadcast([D, HEADS, D]),
                                                ALU.subtract).then_inc(shifted, 1)

                    def sums(it, j, b):
                        n = (it - 1) * GB + b
                        dve.wait_ge(exp_ready, n + 1)
                        nc.vector.tensor_reduce(den[:, (j + 3) % 4, b * HEADS:(b + 1) * HEADS],
                                                pr[:, (j + 1) % 2, b, :].rearrange("p (h k) -> p h k", h=HEADS),
                                                AX.X, ALU.add).then_inc(den_ready, 1)

                    def body(it, j):
                        g3 = it - 3
                        if holds(it, 0):
                            dve.wait_ge(v_mm, it + 1)
                            need(dve, pv_mm, (it - 3) * GB)
                            nc.vector.tensor_copy(v_sb[:, j % 4, :], psum[:, 2, :]).then_inc(v_ready, 1)
                        if holds(it, 3):
                            dve.wait_ge(den_ready, (g3 + 1) * GB)
                            nc.vector.reciprocal(rden[:], den[:, (j + 1) % 4, :]).then_inc(rden_ready, 1)
                            dve.wait_ge(rden_ready, g3 + 1)
                            dve.wait_ge(ot_rows, g3 + 1)
                            need(dve, res_ready, g3 - 1)
                            nc.vector.tensor_tensor(att[:, (j + 1) % 2, :].rearrange("p (a d) -> p a d", d=HD),
                                                    psum[:, 0, :].rearrange("p (a d) -> p a d", d=HD),
                                                    rden[:].unsqueeze(2).to_broadcast([D, GB * HEADS, HD]),
                                                    ALU.mult).then_inc(att_ready, 1)
                        if holds(it, 1):
                            max_of(it, j, 0)
                            shift(it, j, 0)
                            max_of(it, j, 1)
                            shift(it, j, 1)
                        if holds(it, 3):
                            dve.wait_ge(res_ready, g3 + 1)
                            for b in range(GB):
                                ins = nc.vector.bn_stats(st6[:, b, :], res[:, (j + 1) % 2, b * D:(b + 1) * D])
                            ins.then_inc(stats_ready, 1)
                            dve.wait_ge(stats_ready, g3 + 1)
                            nc.vector.tensor_copy(tick[:, 1:2], tick[:, 0:1])
                            for b in range(GB):
                                ins = nc.vector.bn_aggr(mv[:, (j + 1) % 2, b, :], st6[:, b, :])
                            ins.then_inc(moments_ready, 1)
                        if holds(it, 1):
                            max_of(it, j, 2)
                            shift(it, j, 2)
                            sums(it, j, 0)
                            max_of(it, j, 3)
                            shift(it, j, 3)
                            sums(it, j, 1)
                        if holds(it, 4):
                            dve.wait_ge(h2_mm, it - 3)
                            need(dve, h2_ready, it - 4)
                            nc.vector.tensor_tensor(h2a[:, j % 2, :].rearrange("p (b t) -> p b t", b=GB),
                                                    psum[:, 2, :].rearrange("p (b t) -> p b t", b=GB),
                                                    bias1[:].unsqueeze(1).to_broadcast([D, GB, D]),
                                                    ALU.add).then_inc(h2_added, 1)
                        if holds(it, 1):
                            sums(it, j, 2)
                            sums(it, j, 3)
                        if holds(it, 3):
                            dve.wait_ge(h1_mm, g3 + 1)
                            need(dve, h1_ready, g3 - 1)
                            nc.vector.tensor_tensor(h1a[:, (j + 1) % 2, :].rearrange("p (b t) -> p b t", b=GB),
                                                    psum[:, 1, :].rearrange("p (b t) -> p b t", b=GB),
                                                    bias0[:].unsqueeze(1).to_broadcast([D, GB, D]),
                                                    ALU.add).then_inc(h1_added, 1)

                    iterations(dve, body)

                @block.gpsimd
                def _(pool):
                    nc.gpsimd.memset(k_sb[:], 0.0).then_inc(k_zeroed, 1)
                    nc.gpsimd.memset(minus_half[:], -0.5).then_inc(half_set, 1)
                    nc.gpsimd.memset(eps[:], EPS).then_inc(half_set, 1)
                    nc.gpsimd.memset(tock[:], 0.0).then_inc(half_set, 1)
                    pool.wait_ge(half_set, 3)
                    for n in range(6):
                        p, part = n // 2, n % 2
                        pool.wait_ge(w_in[n % 2], 16 * (n // 2 + 1))
                        nc.gpsimd.tensor_copy(w_hi[:, p, part, :], w_raw[:, n % 2, :]).then_inc(w_hi_done, 1)
                        pool.wait_ge(w_hi_done, n + 1)
                        nc.gpsimd.tensor_tensor(w_lo[:, p, part, :], w_raw[:, n % 2, :],
                                                w_hi[:, p, part, :].bitcast(F32), ALU.subtract).then_inc(w_split, 1)

                    def body(it, j):
                        g3 = it - 3
                        s3 = (j + 1) % 2
                        if holds(it, 3):
                            pool.wait_ge(att_ready, g3 + 1)
                            pool.wait_ge(xr_in[s3], slot_dmas(it, j, 3) + 16)
                            need(pool, moments_ready, g3 - 1)
                            nc.gpsimd.tensor_tensor(res[:, s3, :], att[:, s3, :], xr[:, s3, :], ALU.add).then_inc(res_ready, 1)
                            pool.wait_ge(moments_ready, g3 + 1)
                            nc.gpsimd.tensor_tensor(veps[:, s3, :], mv[:, s3, :, 1], eps[:, 0:GB], ALU.add).then_inc(veps_ready, 1)
                            pool.wait_ge(veps_ready, g3 + 1)
                            nc.gpsimd.tensor_tensor(rstd[:, s3, :], veps[:, s3, :], minus_half[:, 0:GB], ALU.pow).then_inc(rstd_ready, 1)
                            pool.wait_ge(rstd_ready, g3 + 1)
                            need(pool, y1_mm, g3 - 1)
                            need(pool, x1_kept[s3], slot_dmas(it, j, 3))
                            nc.gpsimd.tensor_tensor(tock[:, 1:2], tock[:, 0:1], tock[:, 0:1], ALU.add)
                            for b in range(GB):
                                ins = nc.gpsimd.tensor_scalar(x1[:, s3, b * D:(b + 1) * D], res[:, s3, b * D:(b + 1) * D],
                                                              mv[:, s3, b, 0:1], rstd[:, s3, b:b + 1], ALU.subtract, ALU.mult)
                            ins.then_inc(x1_ready, 1)

                    iterations(pool, body)

        with ExitStack() as ctx:
            def s2(name, shape, dt=F32):
                return [sb(f"{name}{c}", shape, dt, ctx) for c in range(2)]

            h_all = s2("h_all", [D, UB, D])
            h_split = s2("h_split", [D, 2, UB, D], F32R)
            h_step = s2("h_step", [D, GW])
            h_step_split = s2("h_step_split", [D, 2, GW], F32R)
            gates = s2("gates", [D, 4, GW])
            cell = s2("cell", [D, GW])
            ig = s2("ig", [D, GW])
            fc = s2("fc", [D, GW])
            tanh_c = s2("tanh_c", [D, GW])
            res2 = s2("res2", [D, 2, GW])
            st6 = s2("st6_", [D, 2 * GB, 6])
            mv = s2("mv_", [D, 2 * GB, 2])
            veps = s2("veps_", [D, 2 * GB])
            rstd = s2("rstd_", [D, 2 * GB])
            out_sb = s2("out_sb", [D, 2, GW])

            def sems2(name):
                return [sem(f"{name}{c}") for c in range(2)]

            gate_mm, gate_ready = sems2("gate_mm"), sems2("gate_ready")
            prod_ready, cell_ready, tanh_ready, h_ready, hi_ready, split_ready = (
                sems2("prod_ready"), sems2("cell_ready"), sems2("tanh_ready"), sems2("h_ready"),
                sems2("hi_ready"), sems2("split_ready"))
            veps2_ready = sems2("veps2_ready")
            rows_mm, res2_ready, stats2_ready, moments2_ready, rstd2_ready, out_ready, out_sent = (
                sems2("rows_mm"), sems2("res2_ready"), sems2("stats2_ready"), sems2("moments2_ready"),
                sems2("rstd2_ready"), sems2("out_ready"), sems2("out_sent"))

            n_slots = len(slots)
            gates_before = [sum(len(slot_gates(s)) for _, s, _ in slots[:k]) for k in range(n_slots + 1)]
            n_gates = gates_before[-1]
            splits = n_slots - 1
            prods_before = [sum(2 for _, s, _ in slots[:k] if s > 0) for k in range(n_slots + 1)]
            n_prods = prods_before[-1]

            def gate_user(k, gate):
                for kk in range(k - 1, -1, -1):
                    if gate in slot_gates(slots[kk][1]):
                        return gates_before[kk] + slot_gates(slots[kk][1]).index(gate) + 1
                return None

            def width(slot):
                p, _, half = slot
                return GW if half is not None else UB * (D // p)

            def in_windows(ap, p, s):
                return ap[..., s:D // p * p:p] if D % p else ap[..., s::p]

            def shaped(ap, slot):
                p, _, half = slot
                b = UB // 2 if half is not None else UB
                return ap[:, 0:width(slot)].rearrange("p (b w) -> p b w", b=b)

            def h_view(ap, slot):
                p, s, half = slot
                if half is not None:
                    return ap[:, half * UB // 2:(half + 1) * UB // 2, :]
                return ap[:, :, s:D // p * p - p + s + 1:p]

            n_pairs = units // 2
            with nc.Block() as block:
                @block.tensor
                def _(pe):
                    def products(c, i, k):
                        slot = slots[k]
                        p, s, half = slot
                        n = width(slot)
                        order = slot_gates(s)
                        base = i * n_gates
                        if s == 0 and p > 1:
                            pe.wait_ge(split_ready[c], i * splits + k)
                        for gate in order:
                            last = gate_user(k, gate)
                            if last is not None:
                                pe.wait_ge(gate_ready[c], base + last)
                            bank = psum[:, 4 * c + gate, 0:n]
                            w = slice(gate * D, (gate + 1) * D)
                            if p == 1:
                                col = bass.ds(i * (2 * UW) + (c * UW + half * GW), GW)
                                nc.tensor.matmul(bank, w_in1[:, w], h2_cols[:, col],
                                                 start=True, stop=True).then_inc(gate_mm[c], 1)
                                continue
                            parts = [(w_hi, 0), (w_hi, 1), (w_lo, 0)]
                            for m, (wt, half_of) in enumerate(parts):
                                mm = nc.tensor.matmul(shaped(bank, slot), wt[:, p - 2, 0, w], h_view(h_split[c][:, half_of], slot),
                                                      start=(m == 0), stop=(s == 0 and m == 2))
                            if s == 0:
                                mm.then_inc(gate_mm[c], 1)
                        if s > 0:
                            pe.wait_ge(split_ready[c], i * splits + k)
                            for gate in order:
                                bank = psum[:, 4 * c + gate, 0:n]
                                w = slice(gate * D, (gate + 1) * D)
                                for m, (wt, half_of) in enumerate([(w_hi, 0), (w_hi, 1), (w_lo, 0)]):
                                    mm = nc.tensor.matmul(bank, wt[:, p - 2, 1, w], h_step_split[c][:, half_of, 0:n],
                                                          start=False, stop=(m == 2))
                                mm.then_inc(gate_mm[c], 1)

                    def rows(c, i):
                        pe.wait_ge(h_ready[c], (i + 1) * n_slots)
                        pe.wait_ge(gate_ready[c], (i + 1) * n_gates)
                        for half in range(2):
                            for b in range(GB):
                                mm = nc.tensor.transpose(psum[:, 4 * c + 2 * half, b * D:(b + 1) * D],
                                                         h_all[c][:, half * GB + b, :], ident[:])
                        mm.then_inc(rows_mm[c], 1)

                    with pe.Fori(0, n_pairs) as i:
                        for k in range(n_slots):
                            for c in range(2):
                                products(c, i, k)
                        for c in range(2):
                            rows(c, i)
                        for c in range(2):
                            pe.wait_ge(res2_ready[c], i + 1)

                @block.scalar
                def _(act):
                    with act.Fori(0, n_pairs) as i:
                        for k, slot in enumerate(slots):
                            p, s, half = slot
                            n = width(slot)
                            for c in range(2):
                                order = slot_gates(s)
                                for m, gate in enumerate(order):
                                    if k > 0 and m == 0:
                                        act.wait_ge(cell_ready[c], i * n_slots + k)
                                    if k > 0 and gate == GATE_O:
                                        act.wait_ge(h_ready[c], i * n_slots + k)
                                    act.wait_ge(gate_mm[c], i * n_gates + (gates_before[k] + m + 1))
                                    nc.scalar.activation(gates[c][:, gate, 0:n], psum[:, 4 * c + gate, 0:n],
                                                         ACT.Tanh if gate == GATE_G else ACT.Sigmoid,
                                                         bias=b_lstm[:, p - 1, gate:gate + 1]).then_inc(gate_ready[c], 1)
                                act.wait_ge(cell_ready[c], i * n_slots + (k + 1))
                                nc.scalar.activation(tanh_c[c][:, 0:n], cell[c][:, 0:n], ACT.Tanh).then_inc(tanh_ready[c], 1)

                @block.vector
                def _(dve):
                    with dve.Fori(0, n_pairs) as i:
                        for k, slot in enumerate(slots):
                            p, s, half = slot
                            n = width(slot)
                            for c in range(2):
                                g_in = gates[c][:, :, 0:n]
                                order = slot_gates(s)
                                if s == 0:
                                    dve.wait_ge(gate_ready[c], i * n_gates + (gates_before[k] + 2))
                                    nc.vector.tensor_tensor(cell[c][:, 0:n], g_in[:, GATE_I], g_in[:, GATE_G],
                                                            ALU.mult).then_inc(cell_ready[c], 1)
                                else:
                                    dve.wait_ge(gate_ready[c], i * n_gates + (gates_before[k] + 2))
                                    nc.vector.tensor_tensor(ig[c][:, 0:n], g_in[:, GATE_I], g_in[:, GATE_G],
                                                            ALU.mult).then_inc(prod_ready[c], 1)
                                    dve.wait_ge(gate_ready[c], i * n_gates + (gates_before[k] + 3))
                                    nc.vector.tensor_tensor(fc[c][:, 0:n], g_in[:, GATE_F], cell[c][:, 0:n],
                                                            ALU.mult).then_inc(prod_ready[c], 1)
                                    dve.wait_ge(prod_ready[c], i * n_prods + prods_before[k + 1])
                                    nc.vector.tensor_tensor(cell[c][:, 0:n], ig[c][:, 0:n], fc[c][:, 0:n],
                                                            ALU.add).then_inc(cell_ready[c], 1)
                                dve.wait_ge(tanh_ready[c], i * n_slots + (k + 1))
                                dve.wait_ge(gate_ready[c], i * n_gates + gates_before[k + 1])
                                if s == p - 1:
                                    h32 = h_view(h_all[c], slot)
                                    hi, lo = (h_view(h_split[c][:, x], slot) for x in range(2))
                                else:
                                    h32 = shaped(h_step[c], slot)
                                    hi, lo = (shaped(h_step_split[c][:, x], slot) for x in range(2))
                                nc.vector.tensor_tensor(h32, shaped(g_in[:, GATE_O], slot), shaped(tanh_c[c], slot),
                                                        ALU.mult).then_inc(h_ready[c], 1)
                                if k < n_slots - 1:
                                    dve.wait_ge(h_ready[c], i * n_slots + (k + 1))
                                    nc.vector.tensor_copy(hi, h32).then_inc(hi_ready[c], 1)
                                    dve.wait_ge(hi_ready[c], i * splits + (k + 1))
                                    nc.vector.tensor_tensor(lo, h32, hi.bitcast(F32), ALU.subtract).then_inc(split_ready[c], 1)
                        for c in range(2):
                            dve.wait_ge(out_ready[c], i + 1)
                            dve.wait_ge(rows_mm[c], i + 1)
                            for half in range(2):
                                col = bass.ds(i * (2 * UW) + (c * UW + half * GW), GW)
                                ins = nc.vector.tensor_tensor(res2[c][:, half, :], psum[:, 4 * c + 2 * half, :],
                                                              x1_rows[:, col], ALU.add)
                            ins.then_inc(res2_ready[c], 1)
                            dve.wait_ge(res2_ready[c], i + 1)
                            for b in range(2 * GB):
                                ins = nc.vector.bn_stats(st6[c][:, b, :], res2[c][:, b // GB, b % GB * D:(b % GB + 1) * D])
                            ins.then_inc(stats2_ready[c], 1)
                            dve.wait_ge(stats2_ready[c], i + 1)
                            nc.vector.tensor_copy(tick[:, 1:2], tick[:, 0:1])
                            for b in range(2 * GB):
                                ins = nc.vector.bn_aggr(mv[c][:, b, :], st6[c][:, b, :])
                            ins.then_inc(moments2_ready[c], 1)

                @block.gpsimd
                def _(pool):
                    for c in range(2):
                        nc.gpsimd.memset(out_sb[c][:, 0, 0:1], 0.0).then_inc(out_ready[c], 1)
                    with pool.Fori(0, n_pairs) as i:
                        for c in range(2):
                            pool.wait_ge(moments2_ready[c], i + 1)
                            nc.gpsimd.tensor_tensor(veps[c][:], mv[c][:, :, 1], eps[:], ALU.add).then_inc(veps2_ready[c], 1)
                            pool.wait_ge(veps2_ready[c], i + 1)
                            nc.gpsimd.tensor_tensor(rstd[c][:], veps[c][:], minus_half[:], ALU.pow).then_inc(rstd2_ready[c], 1)
                            pool.wait_ge(rstd2_ready[c], i + 1)
                            nc.gpsimd.tensor_tensor(tock[:, 1:2], tock[:, 0:1], tock[:, 0:1], ALU.add)
                            for b in range(2 * GB):
                                at = slice(b % GB * D, (b % GB + 1) * D)
                                ins = nc.gpsimd.tensor_scalar(out_sb[c][:, b // GB, at], res2[c][:, b // GB, at],
                                                              mv[c][:, b, 0:1], rstd[c][:, b:b + 1], ALU.subtract, ALU.mult)
                            ins.then_inc(out_ready[c], 1)
                        for c in range(2):
                            pool.wait_ge(out_sent[c], i * 16 + 16)

                @block.sync
                def _(sp):
                    with sp.Fori(0, n_pairs) as i:
                        for c in range(2):
                            at = sp.snap(i * (2 * UW) + c * UW)
                            sp.wait_ge(out_ready[c], i + 2)
                            sp.dma_start(out[:, bass.ds(at, UW)],
                                         out_sb[c][:].rearrange("p a b -> p (a b)")).then_inc(out_sent[c], 16)
                    for c in range(2):
                        sp.wait_ge(out_sent[c], 16 * n_pairs)


def kernel(x, adj, L0_gnn_W, L1_gnn_Wg0, L1_gnn_bg0, L1_gnn_Wg1, L1_gnn_bg1,
           L1_gnn_Wih, L1_gnn_Whh, L1_gnn_bih, L1_gnn_bhh):
    import numpy as np
    import concourse.bacc as bacc
    from concourse.bass_utils import run_bass_kernel_spmd

    x, adj = np.asarray(x), np.asarray(adj)
    batches, nodes, feats = x.shape
    arrays = {
        "x_cols": x.transpose(2, 0, 1).reshape(feats, batches * nodes),
        "x_rows": x.transpose(1, 0, 2).reshape(nodes, batches * feats),
        "adj": adj,
        "adj_t": adj.T,
        "w_qkv": np.asarray(L0_gnn_W),
        "w_g0": np.asarray(L1_gnn_Wg0),
        "b_g0": np.broadcast_to(np.asarray(L1_gnn_bg0)[None, :], (nodes, feats)),
        "w_g1": np.asarray(L1_gnn_Wg1),
        "b_g1": np.asarray(L1_gnn_bg1)[:, None],
        "w_ih": np.asarray(L1_gnn_Wih).transpose(2, 0, 1),
        "w_hh": np.asarray(L1_gnn_Whh).transpose(2, 0, 1),
        "b_ih": np.asarray(L1_gnn_bih).reshape(-1, 4, feats).transpose(2, 0, 1),
        "b_hh": np.asarray(L1_gnn_bhh).reshape(-1, 4, feats).transpose(2, 0, 1),
        "eye": np.eye(feats, dtype=np.float32),
    }
    arrays = {name: np.ascontiguousarray(a) for name, a in arrays.items()}
    nc = bacc.Bacc("TRN2", target_bir_lowering=False, num_devices=1)
    args = [nc.dram_tensor(name, a.shape, mybir.dt.from_np(a.dtype), kind="ExternalInput").ap()
            for name, a in arrays.items()]
    out = nc.dram_tensor("out", (nodes, batches * feats), F32, kind="ExternalOutput").ap()
    adjacent_residual_kernel(nc, *args, out)
    result = run_bass_kernel_spmd(nc, [arrays], core_ids=[0])
    rows = result.results[0]["out"]
    return rows.reshape(nodes, batches, feats).transpose(1, 0, 2)
```

```python
from contextlib import ExitStack

import concourse.bass as bass
from concourse import mybir

F32 = mybir.dt.float32
F32R = mybir.dt.float32r
BF16 = mybir.dt.bfloat16
ALU = mybir.AluOpType
ACT = mybir.ActivationFunctionType
AX = mybir.AxisListType

D = 128
HEADS = 4
HD = D // HEADS
GB = 4
GW = GB * D
EPS = 1e-5
MASKED = -1e30
ATTN_LAG = 4
UNROLL = 4

UB = 8
UW = UB * D
MAX_SKIP = 4
GATE_I, GATE_F, GATE_G, GATE_O = range(4)


def need(eng, sem, n):
    if isinstance(n, int) and n <= 0:
        return
    eng.wait_ge(sem, n)


def lstm_slots():
    slots = [(1, 0, 0), (1, 0, 1)]
    for p in range(2, MAX_SKIP + 1):
        slots += [(p, s, None) for s in range(p)]
    return slots


def slot_gates(step):
    return [GATE_I, GATE_G, GATE_O] if step == 0 else [GATE_I, GATE_G, GATE_F, GATE_O]


def adjacent_residual_kernel(nc, x_cols, x_rows, adj, adj_t, w_qkv, w_g0, b_g0, w_g1, b_g1,
                             w_ih, w_hh, b_ih, b_hh, eye, out):
    n_cols = x_cols.shape[1]
    groups = n_cols // GW
    units = n_cols // UW
    slots = lstm_slots()

    with ExitStack() as top:
        def sb(name, shape, dt=F32, ctx=top):
            return ctx.enter_context(nc.sbuf_tensor(name, shape, dt))

        def sem(name):
            return top.enter_context(nc.semaphore(name))

        psum = top.enter_context(nc.psum_tensor("psum", [D, 8, GW], F32))

        h2_cols = sb("h2_cols", [D, n_cols])
        x1_rows = sb("x1_rows", [D, n_cols])
        ident = sb("ident", [D, D])
        w_in1 = sb("w_in1", [D, 4 * D])
        w_hi = sb("w_hi", [D, 3, 2, 4 * D], F32R)
        w_lo = sb("w_lo", [D, 3, 2, 4 * D], F32R)
        tick = sb("tick", [D, 2])
        zero = sb("zero", [D, 2 * GB])
        eps = sb("eps", [D, 2 * GB])
        minus_half = sb("minus_half", [D, 2 * GB])
        b_lstm = sb("b_lstm", [D, MAX_SKIP, 4])

        with ExitStack() as ctx:
            def s1(name, shape, dt=F32):
                return sb(name, shape, dt, ctx)

            xt = s1("xt", [D, 2, GW])
            xr = s1("xr", [D, 2, GW])
            wq = s1("wq", [D, 3 * D])
            wg0 = s1("wg0", [D, D])
            wg1 = s1("wg1", [D, D])
            adj_sb = s1("adj_sb", [D, D])
            adjt_sb = s1("adjt_sb", [D, D])
            bg0 = s1("bg0", [D, D])
            bg1 = s1("bg1", [D, 1])
            b_raw = s1("b_raw", [D, 2, MAX_SKIP, 4])
            w_raw = s1("w_raw", [D, 2, 4 * D])
            ident_bf = s1("ident_bf", [D, D], BF16)
            mask_bf = s1("mask_bf", [D, HEADS, D], BF16)
            ones = s1("ones", [D, D])
            deg_col = s1("deg_col", [D, 1])
            bias0 = s1("bias0", [D, D])
            bias1 = s1("bias1", [D, D])
            q_sb = s1("q_sb", [D, 2, GW])
            k_sb = s1("k_sb", [D, 2, HEADS, GW])
            v_sb = s1("v_sb", [D, 4, GW])
            sc = s1("sc", [D, 2, GW])
            mx = s1("mx", [D, 2, HEADS])
            pr = s1("pr", [D, 2, GB, GW])
            den = s1("den", [D, 4, GB * HEADS])
            rden = s1("rden", [D, GB * HEADS])
            pt = s1("pt", [D, 2, GW])
            ot = s1("ot", [D, 2, GW])
            att = s1("att", [D, 2, GW])
            res = s1("res", [D, 2, GW])
            st6 = s1("st6", [D, GB, 6])
            mv = s1("mv", [D, 2, GB, 2])
            veps = s1("veps", [D, 2, GB])
            rstd = s1("rstd", [D, 2, GB])
            nmr = s1("nmr", [D, 2, GB])
            neg_mean = s1("neg_mean", [D, GB])
            x1 = s1("x1", [D, 2, GW])
            y1 = s1("y1", [D, 2, GW])
            h1a = s1("h1a", [D, 2, GW])
            h1 = s1("h1", [D, 2, GW])
            y2 = s1("y2", [D, 2, GW])
            h2a = s1("h2a", [D, 2, GW])

            wq_in, consts_in = sem("wq_in"), sem("consts_in")
            xt_in = [sem("xt_in0"), sem("xt_in1")]
            xr_in = [sem("xr_in0"), sem("xr_in1")]
            w_in = [sem("w_in0"), sem("w_in1s")]
            w1_in = sem("w1_in")
            x1_kept = [sem("x1_kept0"), sem("x1_kept1")]
            k_zeroed = sem("k_zeroed")
            setup_dve = sem("setup_dve")
            mask_ready = sem("mask_ready")
            bias1_ready = sem("bias1_ready")
            ones_ready = sem("ones_ready")
            degree_mm = sem("degree_mm")
            w_hi_done, w_split = sem("w_hi_done"), sem("w_split")
            q_mm, k_mm, v_mm = sem("q_mm"), sem("k_mm"), sem("v_mm")
            q_ready, k_ready, v_ready = sem("q_ready"), sem("k_ready"), sem("v_ready")
            score_mm, max_ready, shifted, exp_ready = sem("score_mm"), sem("max_ready"), sem("shifted"), sem("exp_ready")
            den_ready = sem("den_ready")
            pt_mm, pt_ready, pv_mm, ot_ready, ot_rows = sem("pt_mm"), sem("pt_ready"), sem("pv_mm"), sem("ot_ready"), sem("ot_rows")
            rden_ready, att_ready, res_ready, stats_ready, moments_ready = (
                sem("rden_ready"), sem("att_ready"), sem("res_ready"), sem("stats_ready"), sem("moments_ready"))
            half_set, veps_ready = sem("half_set"), sem("veps_ready")
            neg_ready, shift_ready = sem("neg_ready"), sem("shift_ready")
            rstd_ready, x1_ready = sem("rstd_ready"), sem("x1_ready")
            y1_mm, y1_ready, h1_mm, h1_added, h1_ready = (
                sem("y1_mm"), sem("y1_ready"), sem("h1_mm"), sem("h1_added"), sem("h1_ready"))
            y2_mm, y2_ready, h2_mm, h2_added, h2_ready = (
                sem("y2_mm"), sem("y2_ready"), sem("h2_mm"), sem("h2_added"), sem("h2_ready"))

            def holds(it, lag):
                return not isinstance(it, int) or 0 <= it - lag < groups

            def iterations(eng, body):
                begin = ATTN_LAG + 1
                turns = (groups - begin) // UNROLL
                for it in range(begin):
                    body(it, it % UNROLL)
                with eng.Fori(0, turns) as turn:
                    for it in range(begin, begin + UNROLL):
                        body(turn * UNROLL + it, it % UNROLL)
                for it in range(begin + turns * UNROLL, groups + ATTN_LAG):
                    body(it, it % UNROLL)

            def slot_dmas(it, j, lag):
                return (it - j) * 8 + 16 * ((j - lag) // 2)

            def cols(g, width=GW):
                return bass.ds(g * width, width)

            with nc.Block() as block:
                @block.sync
                def _(sp):
                    def body(it, j):
                        fixed = isinstance(it, int)
                        used = it - 1 if fixed else sp.snap(it - 1)
                        passed = it - 3 if fixed else sp.snap(it - 3)
                        at, at2 = ((it - lag) * GW if fixed else sp.snap((it - lag) * GW) for lag in (0, 2))
                        if holds(it, 0):
                            need(sp, v_mm, used)
                            sp.dma_start(xt[:, j % 2], x_cols[:, bass.ds(at, GW)]).then_inc(xt_in[j % 2], 16)
                        if isinstance(it, int) and it == 0:
                            for dst, src in ((adjt_sb[:], adj_t), (adj_sb[:], adj), (ident[:], eye), (wg0[:], w_g0), (wg1[:], w_g1),
                                             (bg0[:], b_g0), (bg1[:], b_g1), (b_raw[:, 0], b_ih), (b_raw[:, 1], b_hh)):
                                sp.dma_start(dst, src).then_inc(consts_in, 16)
                        if isinstance(it, int) and 1 <= it <= 3:
                            if it == 3:
                                sp.dma_start(w_in1[:], w_ih[:, 0]).then_inc(w1_in, 16)
                            for n in (2 * it - 2, 2 * it - 1):
                                need(sp, w_split, n - 1)
                                src = (w_ih if n % 2 == 0 else w_hh)[:, 1 + n // 2]
                                sp.dma_start(w_raw[:, n % 2], src).then_inc(w_in[n % 2], 16)
                        if holds(it, 2):
                            need(sp, res_ready, passed)
                            sp.dma_start(xr[:, j % 2], x_rows[:, bass.ds(at2, GW)]).then_inc(xr_in[j % 2], 16)

                    sp.dma_start(wq[:], w_qkv).then_inc(wq_in, 16)
                    iterations(sp, body)
                    for s in x1_kept:
                        sp.wait_ge(s, 16 * (groups // 2))
                    sp.wait_ge(w1_in, 16)

                N_CONSTS = 9

                @block.tensor
                def _(pe):
                    def transposes_of_p(it, j, b):
                        n = (it - 2) * GB + b
                        pe.wait_ge(exp_ready, n + 1)
                        need(pe, pt_ready, n - 1)
                        for h in range(HEADS):
                            mm = nc.tensor.transpose(psum[:, 5 + b % 2, h * D:(h + 1) * D],
                                                     pr[:, j % 2, b, h * D:(h + 1) * D], ident[:])
                        mm.then_inc(pt_mm, 1)

                    def probs_times_v(it, j, b):
                        g = it - 2
                        n = g * GB + b
                        pe.wait_ge(pt_ready, n + 1)
                        if b == 0:
                            pe.wait_ge(v_ready, g + 1)
                            need(pe, *((ot_ready, g) if holds(it, 3) else (bias1_ready, 1)))
                        for h in range(HEADS):
                            mm = nc.tensor.matmul(psum[HD * h:HD * h + HD, 7, b * D:(b + 1) * D],
                                                  v_sb[:, (j + 2) % 4, b * D + HD * h:b * D + HD * h + HD],
                                                  pt[:, b % 2, h * D:(h + 1) * D], start=True, stop=True)
                        mm.then_inc(pv_mm, 1)

                    def scores(it, j, b):
                        g = it - 1
                        n = g * GB + b
                        bank = psum[:, 3 + b % 2, :]
                        if b == 0:
                            pe.wait_ge(q_ready, g + 1)
                            pe.wait_ge(k_ready, g + 1)
                        need(pe, shifted, n - 1)
                        nc.tensor.matmul(bank, ident_bf[:], mask_bf[:].rearrange("p h k -> p (h k)"),
                                         start=True, stop=False)
                        nc.tensor.matmul(bank, q_sb[:, (j + 1) % 2, b * D:(b + 1) * D],
                                         k_sb[:, (j + 1) % 2, :, b * D:(b + 1) * D],
                                         start=False, stop=True).then_inc(score_mm, 1)

                    def body(it, j):
                        first, drained = isinstance(it, int) and it == 0, not holds(it, 0)
                        if holds(it, 0):
                            pe.wait_ge(xt_in[j % 2], slot_dmas(it, j, 0) + 16)
                            need(pe, *((y1_ready, it - 3) if holds(it, 4) else (q_ready, it)))
                            nc.tensor.matmul(psum[:, 0, :], wq[:, 0:D], xt[:, j % 2, :],
                                             start=True, stop=True).then_inc(q_mm, 1)
                            need(pe, *((h1_added, it - 3) if holds(it, 4) else (k_ready, it)))
                            nc.tensor.matmul(psum[:, 1, :], wq[:, D:2 * D], xt[:, j % 2, :],
                                             start=True, stop=True).then_inc(k_mm, 1)
                            need(pe, *((h2_added, it - 4) if holds(it, 5) else (v_ready, it)))
                            for b in range(GB):
                                mm = nc.tensor.matmul(psum[:, 2, b * D:(b + 1) * D], xt[:, j % 2, b * D:(b + 1) * D],
                                                      wq[:, 2 * D:3 * D], start=True, stop=True)
                            mm.then_inc(v_mm, 1)
                        if first:
                            pe.wait_ge(consts_in, 16 * N_CONSTS)
                            pe.wait_ge(ones_ready, 1)
                            nc.tensor.matmul(psum[:, 7, 0:D], ones[:], adjt_sb[:], start=True, stop=True).then_inc(degree_mm, 1)
                        if holds(it, 3):
                            g = it - 3
                            pe.wait_ge(ot_ready, g + 1)
                            if drained:
                                need(pe, y1_ready, it - 3)
                            else:
                                pe.wait_ge(q_ready, it + 1)
                            for b in range(GB):
                                mm = nc.tensor.transpose(psum[:, 0, b * D:(b + 1) * D],
                                                         ot[:, (j + 1) % 2, b * D:(b + 1) * D], ident[:])
                            mm.then_inc(ot_rows, 1)
                        if holds(it, 1):
                            if isinstance(it, int) and it == 1:
                                pe.wait_ge(mask_ready, 2)
                            scores(it, j, 0)
                        if holds(it, 2):
                            transposes_of_p(it, j, 0)
                        if holds(it, 1):
                            scores(it, j, 1)
                        if holds(it, 4):
                            g = it - 4
                            pe.wait_ge(h1_ready, g + 1)
                            if not drained:
                                pe.wait_ge(k_ready, it + 1)
                            for b in range(GB):
                                mm = nc.tensor.matmul(psum[:, 1, b * D:(b + 1) * D], h1[:, j % 2, b * D:(b + 1) * D],
                                                      adjt_sb[:], start=True, stop=True)
                            mm.then_inc(y2_mm, 1)
                        if holds(it, 2):
                            transposes_of_p(it, j, 1)
                            probs_times_v(it, j, 0)
                        if holds(it, 1):
                            scores(it, j, 2)
                        if holds(it, 4):
                            g = it - 4
                            pe.wait_ge(y2_ready, g + 1)
                            if drained:
                                need(pe, h2_added, g)
                            else:
                                pe.wait_ge(v_ready, it + 1)
                            nc.tensor.matmul(psum[:, 2, :], wg1[:], y2[:, j % 2, :], start=True, stop=True).then_inc(h2_mm, 1)
                        if holds(it, 2):
                            transposes_of_p(it, j, 2)
                            probs_times_v(it, j, 1)
                        if holds(it, 1):
                            scores(it, j, 3)
                        if holds(it, 3):
                            g = it - 3
                            pe.wait_ge(x1_ready, g + 1)
                            pe.wait_ge(att_ready, g + 1)
                            for b in range(GB):
                                mm = nc.tensor.matmul(psum[:, 0, b * D:(b + 1) * D], x1[:, (j + 1) % 2, b * D:(b + 1) * D],
                                                      adjt_sb[:], start=True, stop=True)
                            mm.then_inc(y1_mm, 1)
                        if holds(it, 2):
                            transposes_of_p(it, j, 3)
                            probs_times_v(it, j, 2)
                        if holds(it, 3):
                            g = it - 3
                            pe.wait_ge(y1_ready, g + 1)
                            if holds(it, 4):
                                pe.wait_ge(y2_ready, it - 3)
                            elif not drained:
                                pe.wait_ge(k_ready, it + 1)
                            for b in range(GB):
                                mm = nc.tensor.matmul(psum[:, 1, b * D:(b + 1) * D], y1[:, (j + 1) % 2, b * D:(b + 1) * D],
                                                      wg0[:], start=True, stop=True)
                            mm.then_inc(h1_mm, 1)
                        if holds(it, 2):
                            probs_times_v(it, j, 3)

                    pe.wait_ge(wq_in, 16)
                    iterations(pe, body)

                @block.scalar
                def _(act):
                    def exps(it, j, b):
                        n = (it - 1) * GB + b
                        act.wait_ge(shifted, n + 1)
                        need(act, pt_mm, n - 7)
                        need(act, den_ready, n - 7)
                        nc.scalar.activation(pr[:, (j + 1) % 2, b, :], sc[:, b % 2, :], ACT.Exp).then_inc(exp_ready, 1)

                    def copies_of_pt(it, b):
                        n = (it - 2) * GB + b
                        act.wait_ge(pt_mm, n + 1)
                        need(act, pv_mm, n - 1)
                        nc.scalar.activation(pt[:, b % 2, :], psum[:, 5 + b % 2, :], ACT.Copy).then_inc(pt_ready, 1)

                    def body(it, j):
                        if holds(it, 0):
                            need(act, score_mm, (it - 1) * GB)
                            act.wait_ge(q_mm, it + 1)
                            nc.scalar.activation(q_sb[:, j % 2, :], psum[:, 0, :], ACT.Copy,
                                                 scale=float(HD) ** -0.5).then_inc(q_ready, 1)
                            act.wait_ge(k_mm, it + 1)
                            for h in range(HEADS):
                                ins = nc.scalar.activation(k_sb[HD * h:HD * h + HD, j % 2, h, :],
                                                           psum[HD * h:HD * h + HD, 1, :], ACT.Copy)
                            ins.then_inc(k_ready, 1)
                        if holds(it, 2):
                            copies_of_pt(it, 0)
                        if holds(it, 1):
                            exps(it, j, 0)
                        if holds(it, 4):
                            act.wait_ge(y2_mm, it - 3)
                            nc.scalar.activation(y2[:, j % 2, :], psum[:, 1, :], ACT.Copy).then_inc(y2_ready, 1)
                        if holds(it, 2):
                            copies_of_pt(it, 1)
                        if holds(it, 1):
                            exps(it, j, 1)
                        if holds(it, 3):
                            g3, s3 = it - 3, (j + 1) % 2
                            need(act, y1_mm, g3 - 1)
                            need(act, x1_kept[s3], slot_dmas(it, j, 3))
                            act.wait_ge(shift_ready, g3 + 1)
                            for b in range(GB):
                                ins = nc.scalar.activation(x1[:, s3, b * D:(b + 1) * D], res[:, s3, b * D:(b + 1) * D],
                                                           ACT.Identity, bias=nmr[:, s3, b:b + 1], scale=rstd[:, s3, b:b + 1])
                            ins.then_inc(x1_ready, 1)
                        if holds(it, 2):
                            copies_of_pt(it, 2)
                        if holds(it, 1):
                            exps(it, j, 2)
                        if holds(it, 3):
                            act.wait_ge(y1_mm, it - 2)
                            need(act, h1_mm, it - 4)
                            nc.scalar.activation(y1[:, (j + 1) % 2, :], psum[:, 0, :], ACT.Copy).then_inc(y1_ready, 1)
                        if holds(it, 2):
                            copies_of_pt(it, 3)
                        if holds(it, 4):
                            act.wait_ge(h2_added, it - 3)
                            nc.scalar.activation(h2_cols[:, cols(it - 4)], h2a[:, j % 2, :], ACT.Relu).then_inc(h2_ready, 1)
                            act.wait_ge(x1_ready, it - 3)
                            act.dma_start(x1_rows[:, cols(it - 4)], x1[:, j % 2]).then_inc(x1_kept[j % 2], 16)
                        if holds(it, 1):
                            exps(it, j, 3)
                        if holds(it, 2):
                            act.wait_ge(pv_mm, (it - 1) * GB)
                            need(act, ot_rows, it - 3)
                            nc.scalar.activation(ot[:, j % 2, :], psum[:, 7, :], ACT.Copy).then_inc(ot_ready, 1)
                        if holds(it, 3):
                            act.wait_ge(h1_added, it - 2)
                            need(act, y2_mm, it - 4)
                            nc.scalar.activation(h1[:, (j + 1) % 2, :], h1a[:, (j + 1) % 2, :], ACT.Relu).then_inc(h1_ready, 1)

                    act.wait_ge(k_zeroed, 1)
                    iterations(act, body)

                @block.vector
                def _(dve):
                    dve.wait_ge(consts_in, 16 * N_CONSTS)
                    nc.vector.memset(ones[:], 1.0).then_inc(ones_ready, 1)
                    nc.vector.memset(tick[:], 0.0).then_inc(setup_dve, 1)
                    nc.vector.tensor_copy(ident_bf[:], ident[:]).then_inc(mask_ready, 1)
                    for h in range(HEADS):
                        ins = nc.vector.tensor_scalar(mask_bf[:, h, :], adj_sb[:], 0.0, MASKED, ALU.is_equal, ALU.mult)
                    ins.then_inc(mask_ready, 1)
                    nc.vector.tensor_reduce(deg_col[:], adj_sb[:], AX.X, ALU.add).then_inc(setup_dve, 1)
                    nc.vector.tensor_tensor(b_lstm[:], b_raw[:, 0], b_raw[:, 1], ALU.add)
                    dve.wait_ge(setup_dve, 2)
                    nc.vector.tensor_scalar(bias0[:], bg0[:], deg_col[:, 0:1], None, ALU.mult).then_inc(setup_dve, 1)
                    dve.wait_ge(degree_mm, 1)
                    nc.vector.tensor_scalar(bias1[:], psum[:, 7, 0:D], bg1[:, 0:1], None, ALU.mult).then_inc(bias1_ready, 1)
                    dve.wait_ge(setup_dve, 3)
                    dve.wait_ge(bias1_ready, 1)

                    def max_of(it, j, b):
                        n = (it - 1) * GB + b
                        dve.wait_ge(score_mm, n + 1)
                        nc.vector.tensor_reduce(mx[:, b % 2, :], psum[:, 3 + b % 2, :].rearrange("p (h k) -> p h k", h=HEADS),
                                                AX.X, ALU.max).then_inc(max_ready, 1)

                    def shift(it, j, b):
                        n = (it - 1) * GB + b
                        dve.wait_ge(max_ready, n + 1)
                        need(dve, exp_ready, n - 1)
                        nc.vector.tensor_tensor(sc[:, b % 2, :].rearrange("p (h k) -> p h k", h=HEADS),
                                                psum[:, 3 + b % 2, :].rearrange("p (h k) -> p h k", h=HEADS),
                                                mx[:, b % 2, :].unsqueeze(2).to_broadcast([D, HEADS, D]),
                                                ALU.subtract).then_inc(shifted, 1)

                    def sums(it, j, b):
                        n = (it - 1) * GB + b
                        dve.wait_ge(exp_ready, n + 1)
                        nc.vector.tensor_reduce(den[:, (j + 3) % 4, b * HEADS:(b + 1) * HEADS],
                                                pr[:, (j + 1) % 2, b, :].rearrange("p (h k) -> p h k", h=HEADS),
                                                AX.X, ALU.add).then_inc(den_ready, 1)

                    def body(it, j):
                        g3 = it - 3
                        if holds(it, 0):
                            dve.wait_ge(v_mm, it + 1)
                            need(dve, pv_mm, (it - 3) * GB)
                            nc.vector.tensor_copy(v_sb[:, j % 4, :], psum[:, 2, :]).then_inc(v_ready, 1)
                        if holds(it, 3):
                            dve.wait_ge(den_ready, (g3 + 1) * GB)
                            nc.vector.reciprocal(rden[:], den[:, (j + 1) % 4, :]).then_inc(rden_ready, 1)
                            dve.wait_ge(rden_ready, g3 + 1)
                            dve.wait_ge(ot_rows, g3 + 1)
                            need(dve, res_ready, g3 - 1)
                            nc.vector.tensor_tensor(att[:, (j + 1) % 2, :].rearrange("p (a d) -> p a d", d=HD),
                                                    psum[:, 0, :].rearrange("p (a d) -> p a d", d=HD),
                                                    rden[:].unsqueeze(2).to_broadcast([D, GB * HEADS, HD]),
                                                    ALU.mult).then_inc(att_ready, 1)
                        if holds(it, 1):
                            max_of(it, j, 0)
                            shift(it, j, 0)
                        if holds(it, 3):
                            dve.wait_ge(res_ready, g3 + 1)
                            for b in range(GB):
                                ins = nc.vector.bn_stats(st6[:, b, :], res[:, (j + 1) % 2, b * D:(b + 1) * D])
                            ins.then_inc(stats_ready, 1)
                        if holds(it, 3):
                            dve.wait_ge(stats_ready, g3 + 1)
                            nc.vector.tensor_copy(tick[:, 1:2], tick[:, 0:1])
                            for b in range(GB):
                                ins = nc.vector.bn_aggr(mv[:, (j + 1) % 2, b, :], st6[:, b, :])
                            ins.then_inc(moments_ready, 1)
                        if holds(it, 1):
                            max_of(it, j, 1)
                            shift(it, j, 1)
                            sums(it, j, 0)
                            max_of(it, j, 2)
                            sums(it, j, 1)
                            shift(it, j, 2)
                        if holds(it, 4):
                            dve.wait_ge(h2_mm, it - 3)
                            need(dve, h2_ready, it - 4)
                            nc.vector.tensor_tensor(h2a[:, j % 2, :].rearrange("p (b t) -> p b t", b=GB),
                                                    psum[:, 2, :].rearrange("p (b t) -> p b t", b=GB),
                                                    bias1[:].unsqueeze(1).to_broadcast([D, GB, D]),
                                                    ALU.add).then_inc(h2_added, 1)
                        if holds(it, 1):
                            max_of(it, j, 3)
                            sums(it, j, 2)
                            shift(it, j, 3)
                        if holds(it, 3):
                            dve.wait_ge(h1_mm, g3 + 1)
                            need(dve, h1_ready, g3 - 1)
                            nc.vector.tensor_tensor(h1a[:, (j + 1) % 2, :].rearrange("p (b t) -> p b t", b=GB),
                                                    psum[:, 1, :].rearrange("p (b t) -> p b t", b=GB),
                                                    bias0[:].unsqueeze(1).to_broadcast([D, GB, D]),
                                                    ALU.add).then_inc(h1_added, 1)
                        if holds(it, 1):
                            sums(it, j, 3)

                    iterations(dve, body)

                @block.gpsimd
                def _(pool):
                    nc.gpsimd.memset(k_sb[:], 0.0).then_inc(k_zeroed, 1)
                    nc.gpsimd.memset(minus_half[:], -0.5).then_inc(half_set, 1)
                    nc.gpsimd.memset(eps[:], EPS).then_inc(half_set, 1)
                    nc.gpsimd.memset(zero[:], 0.0).then_inc(half_set, 1)
                    pool.wait_ge(half_set, 3)
                    for n in range(6):
                        p, part = n // 2, n % 2
                        pool.wait_ge(w_in[n % 2], 16 * (n // 2 + 1))
                        nc.gpsimd.tensor_copy(w_hi[:, p, part, :], w_raw[:, n % 2, :]).then_inc(w_hi_done, 1)
                        pool.wait_ge(w_hi_done, n + 1)
                        nc.gpsimd.tensor_tensor(w_lo[:, p, part, :], w_raw[:, n % 2, :],
                                                w_hi[:, p, part, :].bitcast(F32), ALU.subtract).then_inc(w_split, 1)

                    def body(it, j):
                        g3 = it - 3
                        s3 = (j + 1) % 2
                        if holds(it, 3):
                            pool.wait_ge(att_ready, g3 + 1)
                            pool.wait_ge(xr_in[s3], slot_dmas(it, j, 3) + 16)
                            need(pool, x1_ready, g3 - 1)
                            nc.gpsimd.tensor_tensor(res[:, s3, :], att[:, s3, :], xr[:, s3, :], ALU.add).then_inc(res_ready, 1)
                            pool.wait_ge(moments_ready, g3 + 1)
                            nc.gpsimd.tensor_tensor(veps[:, s3, :], mv[:, s3, :, 1], eps[:, 0:GB], ALU.add).then_inc(veps_ready, 1)
                            nc.gpsimd.tensor_tensor(neg_mean[:], zero[:, 0:GB], mv[:, s3, :, 0], ALU.subtract).then_inc(neg_ready, 1)
                            pool.wait_ge(veps_ready, g3 + 1)
                            need(pool, x1_ready, g3 - 1)
                            nc.gpsimd.tensor_tensor(rstd[:, s3, :], veps[:, s3, :], minus_half[:, 0:GB], ALU.pow).then_inc(rstd_ready, 1)
                            pool.wait_ge(neg_ready, g3 + 1)
                            pool.wait_ge(rstd_ready, g3 + 1)
                            nc.gpsimd.tensor_tensor(nmr[:, s3, :], neg_mean[:], rstd[:, s3, :], ALU.mult).then_inc(shift_ready, 1)

                    iterations(pool, body)

        with ExitStack() as ctx:
            def s2(name, shape, dt=F32):
                return [sb(f"{name}{c}", shape, dt, ctx) for c in range(2)]

            h_all = s2("h_all", [D, UB, D])
            h_split = s2("h_split", [D, 2, UB, D], F32R)
            h_step = s2("h_step", [D, GW])
            h_step_split = s2("h_step_split", [D, 2, GW], F32R)
            gates = s2("gates", [D, 4, GW])
            cell = s2("cell", [D, GW])
            ig = s2("ig", [D, GW])
            fc = s2("fc", [D, GW])
            tanh_c = s2("tanh_c", [D, GW])
            res2 = s2("res2", [D, 2, GW])
            st6 = s2("st6_", [D, 2 * GB, 6])
            mv = s2("mv_", [D, 2 * GB, 2])
            veps = s2("veps_", [D, 2 * GB])
            rstd = s2("rstd_", [D, 2 * GB])
            neg_mean = s2("neg_mean_", [D, 2 * GB])
            nmr = s2("nmr_", [D, 2 * GB])
            out_sb = s2("out_sb", [D, 2, GW])

            def sems2(name):
                return [sem(f"{name}{c}") for c in range(2)]

            gate_mm, gate_ready = sems2("gate_mm"), sems2("gate_ready")
            prod_ready, cell_ready, tanh_ready, h_ready, hi_ready, split_ready = (
                sems2("prod_ready"), sems2("cell_ready"), sems2("tanh_ready"), sems2("h_ready"),
                sems2("hi_ready"), sems2("split_ready"))
            veps2_ready, neg2_ready, shift2_ready = sems2("veps2_ready"), sems2("neg2_ready"), sems2("shift2_ready")
            rows_mm, res2_ready, stats2_ready, moments2_ready, rstd2_ready, out_ready, out_sent = (
                sems2("rows_mm"), sems2("res2_ready"), sems2("stats2_ready"), sems2("moments2_ready"),
                sems2("rstd2_ready"), sems2("out_ready"), sems2("out_sent"))

            n_slots = len(slots)
            gates_before = [sum(len(slot_gates(s)) for _, s, _ in slots[:k]) for k in range(n_slots + 1)]
            n_gates = gates_before[-1]
            splits = n_slots - 1
            prods_before = [sum(2 for _, s, _ in slots[:k] if s > 0) for k in range(n_slots + 1)]
            n_prods = prods_before[-1]

            def gate_user(k, gate):
                for kk in range(k - 1, -1, -1):
                    if gate in slot_gates(slots[kk][1]):
                        return gates_before[kk] + slot_gates(slots[kk][1]).index(gate) + 1
                return None

            def width(slot):
                p, _, half = slot
                return GW if half is not None else UB * (D // p)

            def in_windows(ap, p, s):
                return ap[..., s:D // p * p:p] if D % p else ap[..., s::p]

            def shaped(ap, slot):
                p, _, half = slot
                b = UB // 2 if half is not None else UB
                return ap[:, 0:width(slot)].rearrange("p (b w) -> p b w", b=b)

            def h_view(ap, slot):
                p, s, half = slot
                if half is not None:
                    return ap[:, half * UB // 2:(half + 1) * UB // 2, :]
                return ap[:, :, s:D // p * p - p + s + 1:p]

            n_pairs = units // 2
            EARLY = 4

            def pairs(eng, body, tail):
                body(0, False)
                with eng.Fori(1, n_pairs) as i:
                    body(i, True)
                tail(n_pairs)

            def pair_cols(i, c, half):
                return bass.ds(i * (2 * UW) + (c * UW + half * GW), GW)

            with nc.Block() as block:
                @block.tensor
                def _(pe):
                    def products(c, i, k, with_previous, part):
                        slot = slots[k]
                        p, s, half = slot
                        n = width(slot)
                        order = slot_gates(s)
                        if k == 0 and with_previous:
                            pe.wait_ge(gate_ready[c], i * n_gates)

                        def bank_free(gate):
                            last = gate_user(k, gate)
                            if last is not None:
                                pe.wait_ge(gate_ready[c], i * n_gates + last)
                            elif gate == GATE_F and with_previous:
                                pe.wait_ge(res2_ready[c], i * 2)

                        def product(gate, source, w_part, x_part, **flags):
                            bank = psum[:, 4 * c + gate, 0:n]
                            weights = (w_hi, w_lo)[w_part][:, p - 2, source, gate * D:(gate + 1) * D]
                            if source == 0:
                                return nc.tensor.matmul(shaped(bank, slot), weights, h_view(h_split[c][:, x_part], slot), **flags)
                            return nc.tensor.matmul(bank, weights, h_step_split[c][:, x_part, 0:n], **flags)

                        def input_products(gate):
                            bank_free(gate)
                            product(gate, 0, 0, 0, start=True, stop=False)
                            product(gate, 0, 1, 0, start=False, stop=False)
                            product(gate, 0, 0, 1, start=False, stop=False)

                        if part == "inputs":
                            for gate in (GATE_I, GATE_G, GATE_O):
                                input_products(gate)
                            return
                        if p == 1:
                            for gate in order:
                                bank_free(gate)
                                nc.tensor.matmul(psum[:, 4 * c + gate, 0:n], w_in1[:, gate * D:(gate + 1) * D],
                                                 h2_cols[:, pair_cols(i, c, half)], start=True, stop=True).then_inc(gate_mm[c], 1)
                            return
                        source, opens = (1, False) if s > 0 else (0, True)
                        pe.wait_ge(hi_ready[c], i * splits + k)
                        for gate in order[:2]:
                            if opens:
                                bank_free(gate)
                            product(gate, source, 0, 0, start=opens, stop=False)
                            product(gate, source, 1, 0, start=False, stop=False)
                        if s > 0:
                            input_products(GATE_F)
                        pe.wait_ge(split_ready[c], i * splits + k)
                        for gate in order[:2]:
                            product(gate, source, 0, 1, start=False, stop=True).then_inc(gate_mm[c], 1)
                        for gate in order[2:]:
                            if opens:
                                bank_free(gate)
                            product(gate, source, 0, 0, start=opens, stop=False)
                            product(gate, source, 1, 0, start=False, stop=False)
                            product(gate, source, 0, 1, start=False, stop=True).then_inc(gate_mm[c], 1)

                    def rows(c, i, half, bank):
                        if half == 0:
                            pe.wait_ge(h_ready[c], i * n_slots)
                            pe.wait_ge(gate_ready[c], i * n_gates)
                        elif bank == GATE_F:
                            pe.wait_ge(res2_ready[c], i * 2 - 1)
                        for b in range(GB):
                            mm = nc.tensor.transpose(psum[:, 4 * c + bank, b * D:(b + 1) * D],
                                                     h_all[c][:, half * GB + b, :], ident[:])
                        mm.then_inc(rows_mm[c], 1)

                    def body(i, with_previous):
                        for k in range(n_slots):
                            for c in range(2):
                                if slots[k][1] > 0 and not (c == 0 and slots[k][1] == 1 and k > EARLY):
                                    products(c, i, k, with_previous, "inputs")
                                products(c, i, k, with_previous, "rest")
                                if c == 0 and k >= EARLY and slots[k][1] == 0:
                                    products(0, i, k + 1, with_previous, "inputs")
                                if with_previous and k < 2:
                                    rows(c, i, k, GATE_F)

                    def tail(i):
                        for c in range(2):
                            rows(c, i, 0, GATE_F)
                            rows(c, i, 1, GATE_I)

                    pairs(pe, body, tail)

                @block.scalar
                def _(act):
                    def normalized(c, i, batches):
                        if batches[0] == 0:
                            act.wait_ge(shift2_ready[c], i)
                        for b in batches:
                            at = slice(b % GB * D, (b % GB + 1) * D)
                            ins = nc.scalar.activation(out_sb[c][:, b // GB, at], res2[c][:, b // GB, at], ACT.Identity,
                                                       bias=nmr[c][:, b:b + 1], scale=rstd[c][:, b:b + 1])
                        if batches[-1] == UB - 1:
                            ins.then_inc(out_ready[c], 1)

                    def body(i, with_previous):
                        for k, slot in enumerate(slots):
                            p, s, half = slot
                            n = width(slot)
                            for c in range(2):
                                for m, gate in enumerate(slot_gates(s)):
                                    if k > 0 and m == 0:
                                        act.wait_ge(cell_ready[c], i * n_slots + k)
                                    if k > 0 and gate == GATE_O:
                                        act.wait_ge(h_ready[c], i * n_slots + k)
                                    act.wait_ge(gate_mm[c], i * n_gates + (gates_before[k] + m + 1))
                                    nc.scalar.activation(gates[c][:, gate, 0:n], psum[:, 4 * c + gate, 0:n],
                                                         ACT.Tanh if gate == GATE_G else ACT.Sigmoid,
                                                         bias=b_lstm[:, p - 1, gate:gate + 1]).then_inc(gate_ready[c], 1)
                                act.wait_ge(cell_ready[c], i * n_slots + (k + 1))
                                nc.scalar.activation(tanh_c[c][:, 0:n], cell[c][:, 0:n], ACT.Tanh).then_inc(tanh_ready[c], 1)
                                if with_previous and 5 <= k < 9:
                                    normalized(c, i, range(2 * (k - 5), 2 * (k - 5) + 2))
                        if with_previous:
                            for c in range(2):
                                act.wait_ge(out_sent[c], i * 16)

                    def tail(i):
                        for c in range(2):
                            normalized(c, i, range(UB))

                    pairs(act, body, tail)

                @block.vector
                def _(dve):
                    def residual(c, i, half, bank):
                        dve.wait_ge(rows_mm[c], i * 2 - 1 + half)
                        nc.vector.tensor_tensor(res2[c][:, half, :], psum[:, 4 * c + bank, :],
                                                x1_rows[:, pair_cols(i - 1, c, half)], ALU.add).then_inc(res2_ready[c], 1)

                    def statistics(c, i, half):
                        dve.wait_ge(res2_ready[c], i * 2 - 1 + half)
                        for b in range(half * GB, (half + 1) * GB):
                            ins = nc.vector.bn_stats(st6[c][:, b, :], res2[c][:, half, b % GB * D:(b % GB + 1) * D])
                        ins.then_inc(stats2_ready[c], 1)

                    def moments(c, i):
                        dve.wait_ge(stats2_ready[c], i * 2)
                        nc.vector.tensor_copy(tick[:, 1:2], tick[:, 0:1])
                        for b in range(UB):
                            ins = nc.vector.bn_aggr(mv[c][:, b, :], st6[c][:, b, :])
                        ins.then_inc(moments2_ready[c], 1)

                    def body(i, with_previous):
                        for k, slot in enumerate(slots):
                            p, s, half = slot
                            n = width(slot)
                            for c in range(2):
                                g_in = gates[c][:, :, 0:n]
                                dve.wait_ge(gate_ready[c], i * n_gates + (gates_before[k] + 2))
                                if s == 0:
                                    nc.vector.tensor_tensor(cell[c][:, 0:n], g_in[:, GATE_I], g_in[:, GATE_G],
                                                            ALU.mult).then_inc(cell_ready[c], 1)
                                else:
                                    nc.vector.tensor_tensor(ig[c][:, 0:n], g_in[:, GATE_I], g_in[:, GATE_G],
                                                            ALU.mult).then_inc(prod_ready[c], 1)
                                    dve.wait_ge(gate_ready[c], i * n_gates + (gates_before[k] + 3))
                                    nc.vector.tensor_tensor(fc[c][:, 0:n], g_in[:, GATE_F], cell[c][:, 0:n],
                                                            ALU.mult).then_inc(prod_ready[c], 1)
                                    dve.wait_ge(prod_ready[c], i * n_prods + prods_before[k + 1])
                                    nc.vector.tensor_tensor(cell[c][:, 0:n], ig[c][:, 0:n], fc[c][:, 0:n],
                                                            ALU.add).then_inc(cell_ready[c], 1)
                                if with_previous:
                                    if k < 2:
                                        residual(c, i, k, GATE_F)
                                    elif k < 4:
                                        statistics(c, i, k - 2)
                                    elif k == 4:
                                        moments(c, i)
                                dve.wait_ge(tanh_ready[c], i * n_slots + (k + 1))
                                dve.wait_ge(gate_ready[c], i * n_gates + gates_before[k + 1])
                                if s == p - 1:
                                    h32 = h_view(h_all[c], slot)
                                    hi, lo = (h_view(h_split[c][:, x], slot) for x in range(2))
                                else:
                                    h32 = shaped(h_step[c], slot)
                                    hi, lo = (shaped(h_step_split[c][:, x], slot) for x in range(2))
                                nc.vector.tensor_tensor(h32, shaped(g_in[:, GATE_O], slot), shaped(tanh_c[c], slot),
                                                        ALU.mult).then_inc(h_ready[c], 1)
                                if k < n_slots - 1:
                                    dve.wait_ge(h_ready[c], i * n_slots + (k + 1))
                                    nc.vector.tensor_copy(hi, h32).then_inc(hi_ready[c], 1)
                                    dve.wait_ge(hi_ready[c], i * splits + (k + 1))
                                    nc.vector.tensor_tensor(lo, h32, hi.bitcast(F32), ALU.subtract).then_inc(split_ready[c], 1)
                        if with_previous:
                            for c in range(2):
                                dve.wait_ge(out_ready[c], i)

                    def tail(i):
                        for c in range(2):
                            residual(c, i, 0, GATE_F)
                            residual(c, i, 1, GATE_I)
                            statistics(c, i, 0)
                            statistics(c, i, 1)
                            moments(c, i)

                    pairs(dve, body, tail)

                @block.gpsimd
                def _(pool):
                    with pool.Fori(1, n_pairs + 1) as i:
                        for c in range(2):
                            pool.wait_ge(moments2_ready[c], i)
                            nc.gpsimd.tensor_tensor(veps[c][:], mv[c][:, :, 1], eps[:], ALU.add).then_inc(veps2_ready[c], 1)
                            nc.gpsimd.tensor_tensor(neg_mean[c][:], zero[:], mv[c][:, :, 0], ALU.subtract).then_inc(neg2_ready[c], 1)
                            pool.wait_ge(veps2_ready[c], i)
                            nc.gpsimd.tensor_tensor(rstd[c][:], veps[c][:], minus_half[:], ALU.pow).then_inc(rstd2_ready[c], 1)
                            pool.wait_ge(neg2_ready[c], i)
                            pool.wait_ge(rstd2_ready[c], i)
                            nc.gpsimd.tensor_tensor(nmr[c][:], neg_mean[c][:], rstd[c][:], ALU.mult).then_inc(shift2_ready[c], 1)

                @block.sync
                def _(sp):
                    with sp.Fori(0, n_pairs) as i:
                        for c in range(2):
                            at = sp.snap(i * (2 * UW) + c * UW)
                            sp.wait_ge(out_ready[c], i + 1)
                            sp.dma_start(out[:, bass.ds(at, UW)],
                                         out_sb[c][:].rearrange("p a b -> p (a b)")).then_inc(out_sent[c], 16)
                    for c in range(2):
                        sp.wait_ge(out_sent[c], 16 * n_pairs)


def kernel(x, adj, L0_gnn_W, L1_gnn_Wg0, L1_gnn_bg0, L1_gnn_Wg1, L1_gnn_bg1,
           L1_gnn_Wih, L1_gnn_Whh, L1_gnn_bih, L1_gnn_bhh):
    import numpy as np
    import concourse.bacc as bacc
    from concourse.bass_utils import run_bass_kernel_spmd

    x, adj = np.asarray(x), np.asarray(adj)
    batches, nodes, feats = x.shape
    arrays = {
        "x_cols": x.transpose(2, 0, 1).reshape(feats, batches * nodes),
        "x_rows": x.transpose(1, 0, 2).reshape(nodes, batches * feats),
        "adj": adj,
        "adj_t": adj.T,
        "w_qkv": np.asarray(L0_gnn_W),
        "w_g0": np.asarray(L1_gnn_Wg0),
        "b_g0": np.broadcast_to(np.asarray(L1_gnn_bg0)[None, :], (nodes, feats)),
        "w_g1": np.asarray(L1_gnn_Wg1),
        "b_g1": np.asarray(L1_gnn_bg1)[:, None],
        "w_ih": np.asarray(L1_gnn_Wih).transpose(2, 0, 1),
        "w_hh": np.asarray(L1_gnn_Whh).transpose(2, 0, 1),
        "b_ih": np.asarray(L1_gnn_bih).reshape(-1, 4, feats).transpose(2, 0, 1),
        "b_hh": np.asarray(L1_gnn_bhh).reshape(-1, 4, feats).transpose(2, 0, 1),
        "eye": np.eye(feats, dtype=np.float32),
    }
    arrays = {name: np.ascontiguousarray(a) for name, a in arrays.items()}
    nc = bacc.Bacc("TRN2", target_bir_lowering=False, num_devices=1)
    args = [nc.dram_tensor(name, a.shape, mybir.dt.from_np(a.dtype), kind="ExternalInput").ap()
            for name, a in arrays.items()]
    out = nc.dram_tensor("out", (nodes, batches * feats), F32, kind="ExternalOutput").ap()
    adjacent_residual_kernel(nc, *args, out)
    result = run_bass_kernel_spmd(nc, [arrays], core_ids=[0])
    rows = result.results[0]["out"]
    return rows.reshape(nodes, batches, feats).transpose(1, 0, 2)
```

```python
from contextlib import ExitStack

import concourse.bass as bass
from concourse import mybir

F32 = mybir.dt.float32
F32R = mybir.dt.float32r
BF16 = mybir.dt.bfloat16
ALU = mybir.AluOpType
ACT = mybir.ActivationFunctionType
AX = mybir.AxisListType

D = 128
HEADS = 4
HD = D // HEADS
GB = 4
GW = GB * D
EPS = 1e-5
MASKED = -1e30
ATTN_LAG = 4
UNROLL = 4

UB = 8
UW = UB * D
MAX_SKIP = 4
GATE_I, GATE_F, GATE_G, GATE_O = range(4)
BANK = ((4, 2, 6, 7), (3, 1, 5, 0))


def need(eng, sem, n):
    if isinstance(n, int) and n <= 0:
        return
    eng.wait_ge(sem, n)


def lstm_slots():
    slots = [(1, 0, 0), (1, 0, 1)]
    for p in range(2, MAX_SKIP + 1):
        slots += [(p, s, None) for s in range(p)]
    return slots


def slot_gates(step):
    return [GATE_I, GATE_G, GATE_O] if step == 0 else [GATE_I, GATE_G, GATE_F, GATE_O]


def adjacent_residual_kernel(nc, x_cols, x_rows, adj, adj_t, w_qkv, w_g0, b_g0, w_g1, b_g1,
                             w_ih, w_hh, b_ih, b_hh, eye, out):
    n_cols = x_cols.shape[1]
    groups = n_cols // GW
    units = n_cols // UW
    slots = lstm_slots()

    with ExitStack() as top:
        def sb(name, shape, dt=F32, ctx=top):
            return ctx.enter_context(nc.sbuf_tensor(name, shape, dt))

        def sem(name):
            return top.enter_context(nc.semaphore(name))

        psum = top.enter_context(nc.psum_tensor("psum", [D, 8, GW], F32))

        def sems2(name):
            return [sem(f"{name}{c}") for c in range(2)]

        gate_mm, gate_ready = sems2("gate_mm"), sems2("gate_ready")

        h2_cols = sb("h2_cols", [D, n_cols])
        x1_rows = sb("x1_rows", [D, n_cols])
        ident = sb("ident", [D, D])
        w_in1 = sb("w_in1", [D, 4 * D])
        w_hi = sb("w_hi", [D, 3, 2, 4 * D], F32R)
        w_lo = sb("w_lo", [D, 3, 2, 4 * D], F32R)
        k_sb = gates = [sb(f"k_or_gates{n}", [D, 4, GW]) for n in range(2)]
        tick = sb("tick", [D, 2])
        zero = sb("zero", [D, 2 * GB])
        eps = sb("eps", [D, 2 * GB])
        minus_half = sb("minus_half", [D, 2 * GB])
        b_lstm = sb("b_lstm", [D, MAX_SKIP, 4])

        with ExitStack() as ctx:
            def s1(name, shape, dt=F32):
                return sb(name, shape, dt, ctx)

            xt = s1("xt", [D, 2, GW])
            q_sb = s1("q_sb", [D, 2, GW])
            v_sb = s1("v_sb", [D, 4, GW])
            sc = s1("sc", [D, 2, GW])
            pr = s1("pr", [D, 2, GB, GW])
            pt = s1("pt", [D, 2, GW])
            x_parts = s1("x_parts", [D, 2, GW], F32R)
            wqk_parts = s1("wqk_parts", [D, 2, 2 * D], F32R)
            xr = s1("xr", [D, 2, GW])
            wq = s1("wq", [D, 3 * D])
            wg0 = s1("wg0", [D, D])
            wg1 = s1("wg1", [D, D])
            adj_sb = s1("adj_sb", [D, D])
            adjt_sb = s1("adjt_sb", [D, D])
            bg0 = s1("bg0", [D, D])
            bg1 = s1("bg1", [D, 1])
            b_raw = s1("b_raw", [D, 2, MAX_SKIP, 4])
            w_raw = s1("w_raw", [D, 2, 4 * D])
            ident_bf = s1("ident_bf", [D, D], BF16)
            mask_bf = s1("mask_bf", [D, HEADS, D], BF16)
            ones = s1("ones", [D, D])
            deg_col = s1("deg_col", [D, 1])
            bias0 = s1("bias0", [D, D])
            bias1 = s1("bias1", [D, D])
            mx = s1("mx", [D, 2, HEADS])
            den = s1("den", [D, 4, GB * HEADS])
            rden = s1("rden", [D, GB * HEADS])
            ot = s1("ot", [D, 2, GW])
            att = s1("att", [D, 2, GW])
            res = s1("res", [D, 2, GW])
            st6 = s1("st6", [D, GB, 6])
            mv = s1("mv", [D, 2, GB, 2])
            veps = s1("veps", [D, 2, GB])
            rstd = s1("rstd", [D, 2, GB])
            nmr = s1("nmr", [D, 2, GB])
            neg_mean = s1("neg_mean", [D, GB])
            x1 = s1("x1", [D, 2, GW])
            y1 = s1("y1", [D, 2, GW])
            h1a = s1("h1a", [D, 2, GW])
            h1 = s1("h1", [D, 2, GW])
            y2 = s1("y2", [D, 2, GW])
            h2a = s1("h2a", [D, 2, GW])

            wq_in, consts_in = sem("wq_in"), sem("consts_in")
            xt_in = [sem("xt_in0"), sem("xt_in1")]
            xr_in = [sem("xr_in0"), sem("xr_in1")]
            w_in = [sem("w_in0"), sem("w_in1s")]
            w1_in = sem("w1_in")
            x1_kept = [sem("x1_kept0"), sem("x1_kept1")]
            k_zeroed = sem("k_zeroed")
            setup_dve = sem("setup_dve")
            mask_ready = sem("mask_ready")
            bias1_ready = sem("bias1_ready")
            ones_ready = sem("ones_ready")
            degree_mm = sem("degree_mm")
            w_hi_done, w_split = sem("w_hi_done"), sem("w_split")
            x_hi_done, x_split, wqk_hi_done, wqk_split = sem("x_hi_done"), sem("x_split"), sem("wqk_hi_done"), sem("wqk_split")
            q_mm, k_mm, v_mm = sem("q_mm"), sem("k_mm"), sem("v_mm")
            q_ready, k_ready, v_ready = sem("q_ready"), sem("k_ready"), sem("v_ready")
            score_mm, max_ready, shifted, exp_ready = sem("score_mm"), sem("max_ready"), sem("shifted"), sem("exp_ready")
            den_ready = sem("den_ready")
            pt_mm, pt_ready, pv_mm, ot_ready, ot_rows = sem("pt_mm"), sem("pt_ready"), sem("pv_mm"), sem("ot_ready"), sem("ot_rows")
            rden_ready, att_ready, res_ready, stats_ready, moments_ready = (
                sem("rden_ready"), sem("att_ready"), sem("res_ready"), sem("stats_ready"), sem("moments_ready"))
            half_set, veps_ready = sem("half_set"), sem("veps_ready")
            neg_ready, shift_ready = sem("neg_ready"), sem("shift_ready")
            rstd_ready, x1_ready = sem("rstd_ready"), sem("x1_ready")
            y1_mm, y1_ready, h1_mm, h1_added, h1_ready = (
                sem("y1_mm"), sem("y1_ready"), sem("h1_mm"), sem("h1_added"), sem("h1_ready"))
            y2_mm, y2_ready, h2_mm, h2_added, h2_ready = (
                sem("y2_mm"), sem("y2_ready"), sem("h2_mm"), sem("h2_added"), sem("h2_ready"))

            def holds(it, lag):
                return not isinstance(it, int) or 0 <= it - lag < groups

            def last_with_pv(it):
                return isinstance(it, int) and it == groups + 1

            FIRST_SPLIT = 3

            def in_parts(it):
                return not isinstance(it, int) or it >= FIRST_SPLIT

            def norms(it):
                return holds(it, 3) and not (isinstance(it, int) and it == groups + 2)

            def iterations(eng, body):
                begin = ATTN_LAG + 1
                turns = (groups - begin) // UNROLL
                for it in range(begin):
                    body(it, it % UNROLL)
                with eng.Fori(0, turns) as turn:
                    for it in range(begin, begin + UNROLL):
                        body(turn * UNROLL + it, it % UNROLL)
                for it in range(begin + turns * UNROLL, groups + ATTN_LAG):
                    body(it, it % UNROLL)

            def slot_dmas(it, j, lag):
                return (it - j) * 8 + 16 * ((j - lag) // 2)

            def cols(g, width=GW):
                return bass.ds(g * width, width)

            def phase1_sync(sp):
                def body(it, j):
                    fixed = isinstance(it, int)
                    used = it - 1 if fixed else sp.snap(it - 1)
                    passed = it - 3 if fixed else sp.snap(it - 3)
                    at, at2 = ((it - lag) * GW if fixed else sp.snap((it - lag) * GW) for lag in (0, 2))
                    if holds(it, 0):
                        need(sp, v_mm, used)
                        sp.dma_start(xt[:, j % 2], x_cols[:, bass.ds(at, GW)]).then_inc(xt_in[j % 2], 16)
                    if isinstance(it, int) and it == 0:
                        for dst, src in ((adjt_sb[:], adj_t), (adj_sb[:], adj), (ident[:], eye), (wg0[:], w_g0), (wg1[:], w_g1),
                                         (bg0[:], b_g0), (bg1[:], b_g1), (b_raw[:, 0], b_ih), (b_raw[:, 1], b_hh)):
                            sp.dma_start(dst, src).then_inc(consts_in, 16)
                    if isinstance(it, int) and 1 <= it <= 3:
                        if it == 3:
                            sp.dma_start(w_in1[:], w_ih[:, 0]).then_inc(w1_in, 16)
                        for n in (2 * it - 2, 2 * it - 1):
                            need(sp, w_split, n - 1)
                            src = (w_ih if n % 2 == 0 else w_hh)[:, 1 + n // 2]
                            sp.dma_start(w_raw[:, n % 2], src).then_inc(w_in[n % 2], 16)
                    if holds(it, 2):
                        need(sp, res_ready, passed)
                        sp.dma_start(xr[:, j % 2], x_rows[:, bass.ds(at2, GW)]).then_inc(xr_in[j % 2], 16)

                sp.dma_start(wq[:], w_qkv).then_inc(wq_in, 16)
                iterations(sp, body)
                for s in x1_kept:
                    sp.wait_ge(s, 16 * (groups // 2))
                sp.wait_ge(w1_in, 16)

            N_CONSTS = 9

            def phase1_tensor(pe):
                def transposes_of_p(it, j, b):
                    n = (it - 2) * GB + b
                    pe.wait_ge(exp_ready, n + 1)
                    need(pe, pt_ready, n - 1)
                    for h in range(HEADS):
                        mm = nc.tensor.transpose(psum[:, 5 + b % 2, h * D:(h + 1) * D],
                                                 pr[:, j % 2, b, h * D:(h + 1) * D], ident[:])
                    mm.then_inc(pt_mm, 1)

                def probs_times_v(it, j, b):
                    g = it - 2
                    n = g * GB + b
                    pe.wait_ge(pt_ready, n + 1)
                    if b == 0:
                        pe.wait_ge(v_ready, g + 1)
                        need(pe, *((ot_ready, g) if holds(it, 3) else (bias1_ready, 1)))
                    for h in range(HEADS):
                        mm = nc.tensor.matmul(psum[HD * h:HD * h + HD, 7, b * D:(b + 1) * D],
                                              v_sb[:, (j + 2) % 4, b * D + HD * h:b * D + HD * h + HD],
                                              pt[:, b % 2, h * D:(h + 1) * D], start=True, stop=True)
                    mm.then_inc(pv_mm, 1)

                def scores(it, j, b):
                    g = it - 1
                    n = g * GB + b
                    bank = psum[:, 3 + b % 2, :]
                    if b == 0:
                        pe.wait_ge(q_ready, g + 1)
                        pe.wait_ge(k_ready, g + 1)
                    need(pe, shifted, n - 1)
                    nc.tensor.matmul(bank, ident_bf[:], mask_bf[:].rearrange("p h k -> p (h k)"),
                                     start=True, stop=False)
                    nc.tensor.matmul(bank, q_sb[:, (j + 1) % 2, b * D:(b + 1) * D],
                                     k_sb[(j + 1) % 2][:, :, b * D:(b + 1) * D],
                                     start=False, stop=True).then_inc(score_mm, 1)

                def attention_rows(it, j, drained):
                    g = it - 3
                    pe.wait_ge(ot_ready, g + 1)
                    if not drained:
                        pe.wait_ge(q_ready, it + 1)
                    elif last_with_pv(it - 1):
                        pe.wait_ge(att_ready, g)
                    else:
                        pe.wait_ge(y1_ready, g)
                    for b in range(GB):
                        mm = nc.tensor.transpose(psum[:, 0, b * D:(b + 1) * D],
                                                 ot[:, (j + 1) % 2, b * D:(b + 1) * D], ident[:])
                    mm.then_inc(ot_rows, 1)

                def projection(it, j, which):
                    at = slice(which * D, (which + 1) * D)
                    if not in_parts(it):
                        return nc.tensor.matmul(psum[:, which, :], wq[:, at], xt[:, j % 2, :], start=True, stop=True)
                    for m, (w_part, x_part) in enumerate(((0, 0), (1, 0), (0, 1))):
                        mm = nc.tensor.matmul(psum[:, which, :], wqk_parts[:, w_part, at], x_parts[:, x_part, :],
                                              start=(m == 0), stop=(m == 2))
                    return mm

                def first_layer_y(it, j):
                    g = it - 3
                    pe.wait_ge(x1_ready, g + 1)
                    if not norms(it):
                        pe.wait_ge(y1_ready, g)
                    else:
                        pe.wait_ge(att_ready, g + (2 if last_with_pv(it) else 1))
                    for b in range(GB):
                        mm = nc.tensor.matmul(psum[:, 0, b * D:(b + 1) * D], x1[:, (j + 1) % 2, b * D:(b + 1) * D],
                                              adjt_sb[:], start=True, stop=True)
                    mm.then_inc(y1_mm, 1)

                def first_layer_h(it, j, drained):
                    g = it - 3
                    pe.wait_ge(y1_ready, g + 1)
                    if holds(it, 4):
                        pe.wait_ge(y2_ready, it - 3)
                    elif not drained:
                        pe.wait_ge(k_ready, it + 1)
                    for b in range(GB):
                        mm = nc.tensor.matmul(psum[:, 1, b * D:(b + 1) * D], y1[:, (j + 1) % 2, b * D:(b + 1) * D],
                                              wg0[:], start=True, stop=True)
                    mm.then_inc(h1_mm, 1)

                def second_layer_y(it, j, drained):
                    g = it - 4
                    pe.wait_ge(h1_ready, g + 1)
                    if not drained:
                        pe.wait_ge(k_ready, it + 1)
                    for b in range(GB):
                        mm = nc.tensor.matmul(psum[:, 1, b * D:(b + 1) * D], h1[:, j % 2, b * D:(b + 1) * D],
                                              adjt_sb[:], start=True, stop=True)
                    mm.then_inc(y2_mm, 1)

                def second_layer_h(it, j, drained):
                    g = it - 4
                    pe.wait_ge(y2_ready, g + 1)
                    if drained:
                        need(pe, h2_added, g)
                    else:
                        pe.wait_ge(v_ready, it + 1)
                    nc.tensor.matmul(psum[:, 2, :], wg1[:], y2[:, j % 2, :], start=True, stop=True).then_inc(h2_mm, 1)

                def lstm_product(c, k, gate, bank_read, n):
                    pe.wait_ge(bank_read, n)
                    nc.tensor.matmul(psum[:, BANK[c][gate], :], w_in1[:, gate * D:(gate + 1) * D],
                                     h2_cols[:, cols(UB // GB * c + k)], start=True, stop=True).then_inc(gate_mm[c], 1)

                def body(it, j):
                    first, drained = isinstance(it, int) and it == 0, not holds(it, 0)
                    drained_late = isinstance(it, int) and it > groups + 1
                    if isinstance(it, int) and it > groups + 2:
                        return
                    if holds(it, 0):
                        pe.wait_ge(xt_in[j % 2], slot_dmas(it, j, 0) + 16)
                        need(pe, *((y1_ready, it - 3) if holds(it, 4) else (q_ready, it)))
                        if isinstance(it, int) and it == FIRST_SPLIT:
                            pe.wait_ge(wqk_split, 1)
                        if in_parts(it):
                            pe.wait_ge(x_split, it - (FIRST_SPLIT - 1))
                        projection(it, j, 0).then_inc(q_mm, 1)
                        need(pe, *((h1_added, it - 3) if holds(it, 4) else (k_ready, it)))
                        projection(it, j, 1).then_inc(k_mm, 1)
                        need(pe, *((h2_added, it - 4) if holds(it, 5) else (v_ready, it)))
                        for b in range(GB):
                            mm = nc.tensor.matmul(psum[:, 2, b * D:(b + 1) * D], xt[:, j % 2, b * D:(b + 1) * D],
                                                  wq[:, 2 * D:3 * D], start=True, stop=True)
                        mm.then_inc(v_mm, 1)
                    if first:
                        pe.wait_ge(consts_in, 16 * N_CONSTS)
                        pe.wait_ge(ones_ready, 1)
                        nc.tensor.matmul(psum[:, 7, 0:D], ones[:], adjt_sb[:], start=True, stop=True).then_inc(degree_mm, 1)
                    if norms(it):
                        attention_rows(it, j, drained)
                    if holds(it, 1):
                        if isinstance(it, int) and it == 1:
                            pe.wait_ge(mask_ready, 2)
                        scores(it, j, 0)
                    if holds(it, 2):
                        transposes_of_p(it, j, 0)
                    if holds(it, 1):
                        scores(it, j, 1)
                    if holds(it, 4) and not drained_late:
                        second_layer_y(it, j, drained)
                    if holds(it, 2):
                        transposes_of_p(it, j, 1)
                        probs_times_v(it, j, 0)
                    if holds(it, 1):
                        scores(it, j, 2)
                    if holds(it, 4) and not drained_late:
                        second_layer_h(it, j, drained)
                    if holds(it, 2):
                        transposes_of_p(it, j, 2)
                        probs_times_v(it, j, 1)
                    if holds(it, 1):
                        scores(it, j, 3)
                    if last_with_pv(it):
                        pe.wait_ge(w1_in, 16)
                        pe.wait_ge(h2_ready, UB // GB + 1)
                        transposes_of_p(it, j, 3)
                        probs_times_v(it, j, 2)
                        probs_times_v(it, j, 3)
                        lstm_product(0, 0, GATE_I, shifted, groups * GB)
                        attention_rows(it + 1, j + 1, drained)
                        lstm_product(0, 0, GATE_G, pt_ready, groups * GB)
                    if holds(it, 3) and not drained_late:
                        first_layer_y(it, j)
                    if last_with_pv(it):
                        lstm_product(0, 0, GATE_O, ot_ready, groups)
                    if holds(it, 2) and not last_with_pv(it):
                        transposes_of_p(it, j, 3)
                        probs_times_v(it, j, 2)
                    if holds(it, 3) and not drained_late:
                        first_layer_h(it, j, drained)
                    if drained_late:
                        lstm_product(1, 0, GATE_I, shifted, groups * GB)
                        lstm_product(1, 0, GATE_G, pt_ready, groups * GB)
                        lstm_product(0, 1, GATE_I, gate_ready[0], 1)
                        first_layer_y(it, j)
                        second_layer_y(it, j, drained)
                        lstm_product(0, 1, GATE_G, gate_ready[0], 2)
                        first_layer_h(it, j, drained)
                        lstm_product(1, 0, GATE_O, y1_ready, groups)
                        second_layer_h(it, j, drained)
                        second_layer_y(it + 1, j + 1, drained)
                        lstm_product(0, 1, GATE_O, gate_ready[0], 3)
                        second_layer_h(it + 1, j + 1, drained)
                    if holds(it, 2) and not last_with_pv(it):
                        probs_times_v(it, j, 3)

                pe.wait_ge(wq_in, 16)
                iterations(pe, body)

            def phase1_scalar(act):
                def exps(it, j, b):
                    n = (it - 1) * GB + b
                    act.wait_ge(shifted, n + 1)
                    need(act, pt_mm, n - 7)
                    need(act, den_ready, n - 7)
                    nc.scalar.activation(pr[:, (j + 1) % 2, b, :], sc[:, b % 2, :], ACT.Exp).then_inc(exp_ready, 1)

                def copies_of_pt(it, b):
                    n = (it - 2) * GB + b
                    act.wait_ge(pt_mm, n + 1)
                    need(act, pv_mm, n - 1)
                    nc.scalar.activation(pt[:, b % 2, :], psum[:, 5 + b % 2, :], ACT.Copy).then_inc(pt_ready, 1)

                def copy_of_y2(it, j):
                    act.wait_ge(y2_mm, it - 3)
                    nc.scalar.activation(y2[:, j % 2, :], psum[:, 1, :], ACT.Copy).then_inc(y2_ready, 1)

                def relu_of_h2(it, j):
                    act.wait_ge(h2_added, it - 3)
                    nc.scalar.activation(h2_cols[:, cols(it - 4)], h2a[:, j % 2, :], ACT.Relu).then_inc(h2_ready, 1)

                def store_x1(it, j):
                    act.wait_ge(x1_ready, it - 3)
                    act.dma_start(x1_rows[:, cols(it - 4)], x1[:, j % 2]).then_inc(x1_kept[j % 2], 16)

                def relu_of_h1(it, j):
                    act.wait_ge(h1_added, it - 2)
                    need(act, y2_mm, it - 4)
                    nc.scalar.activation(h1[:, (j + 1) % 2, :], h1a[:, (j + 1) % 2, :], ACT.Relu).then_inc(h1_ready, 1)

                def copy_of_ot(it, j):
                    act.wait_ge(pv_mm, (it - 1) * GB)
                    need(act, ot_rows, it - 3)
                    nc.scalar.activation(ot[:, j % 2, :], psum[:, 7, :], ACT.Copy).then_inc(ot_ready, 1)

                def body(it, j):
                    late = isinstance(it, int) and it >= groups + 2
                    if isinstance(it, int) and it == groups + 3:
                        copy_of_y2(it, j)
                        step_gate(act, 1, 0, 0, 1)
                        step_gate(act, 1, 0, 0, 2)
                        relu_of_h2(it - 1, j - 1)
                        step_tanh(act, 1, 0, 0)
                        relu_of_h2(it, j)
                        return
                    if holds(it, 0):
                        need(act, score_mm, (it - 1) * GB)
                        act.wait_ge(q_mm, it + 1)
                        nc.scalar.activation(q_sb[:, j % 2, :], psum[:, 0, :], ACT.Copy,
                                             scale=float(HD) ** -0.5).then_inc(q_ready, 1)
                        act.wait_ge(k_mm, it + 1)
                        for h in range(HEADS):
                            ins = nc.scalar.activation(k_sb[j % 2][HD * h:HD * h + HD, h, :],
                                                       psum[HD * h:HD * h + HD, 1, :], ACT.Copy)
                        ins.then_inc(k_ready, 1)
                    if holds(it, 2):
                        copies_of_pt(it, 0)
                    if holds(it, 1):
                        exps(it, j, 0)
                    if holds(it, 4) and norms(it):
                        copy_of_y2(it, j)
                    if holds(it, 2):
                        copies_of_pt(it, 1)
                    if holds(it, 1):
                        exps(it, j, 1)
                    if last_with_pv(it):
                        copies_of_pt(it, 2)
                        copies_of_pt(it, 3)
                        copy_of_ot(it, j)
                    if holds(it, 3):
                        g3, s3 = it - 3, (j + 1) % 2
                        need(act, y1_mm, g3 - 1)
                        need(act, x1_kept[s3], slot_dmas(it, j, 3))
                        act.wait_ge(shift_ready, g3 + 1)
                        for b in range(GB):
                            ins = nc.scalar.activation(x1[:, s3, b * D:(b + 1) * D], res[:, s3, b * D:(b + 1) * D],
                                                       ACT.Identity, bias=nmr[:, s3, b:b + 1], scale=rstd[:, s3, b:b + 1])
                        ins.then_inc(x1_ready, 1)
                    if holds(it, 2) and not last_with_pv(it):
                        copies_of_pt(it, 2)
                    if holds(it, 1):
                        exps(it, j, 2)
                    if holds(it, 3):
                        act.wait_ge(y1_mm, it - 2)
                        need(act, h1_mm, it - 4)
                        nc.scalar.activation(y1[:, (j + 1) % 2, :], psum[:, 0, :], ACT.Copy).then_inc(y1_ready, 1)
                    if holds(it, 4) and not norms(it):
                        copy_of_y2(it, j)
                    if holds(it, 2) and not last_with_pv(it):
                        copies_of_pt(it, 3)
                    if late:
                        step_gate(act, 0, 0, 0, 2)
                        relu_of_h1(it, j)
                        step_tanh(act, 0, 0, 0)
                        store_x1(it, j)
                        store_x1(it + 1, j + 1)
                    if holds(it, 4) and not late:
                        relu_of_h2(it, j)
                        store_x1(it, j)
                    if late:
                        step_gate(act, 1, 0, 0, 0)
                    if last_with_pv(it):
                        act.wait_ge(score_mm, groups * GB)
                        step_gate(act, 0, 0, 0, 0)
                    if holds(it, 1):
                        exps(it, j, 3)
                    if holds(it, 2) and not last_with_pv(it):
                        copy_of_ot(it, j)
                    if holds(it, 3) and not late:
                        relu_of_h1(it, j)
                    if last_with_pv(it):
                        step_gate(act, 0, 0, 0, 1)

                act.wait_ge(k_zeroed, 2)
                iterations(act, body)

            def phase1_vector(dve):
                dve.wait_ge(consts_in, 16 * N_CONSTS)
                nc.vector.memset(ones[:], 1.0).then_inc(ones_ready, 1)
                nc.vector.memset(tick[:], 0.0).then_inc(setup_dve, 1)
                nc.vector.tensor_copy(ident_bf[:], ident[:]).then_inc(mask_ready, 1)
                for h in range(HEADS):
                    ins = nc.vector.tensor_scalar(mask_bf[:, h, :], adj_sb[:], 0.0, MASKED, ALU.is_equal, ALU.mult)
                ins.then_inc(mask_ready, 1)
                nc.vector.tensor_reduce(deg_col[:], adj_sb[:], AX.X, ALU.add).then_inc(setup_dve, 1)
                nc.vector.tensor_tensor(b_lstm[:], b_raw[:, 0], b_raw[:, 1], ALU.add)
                dve.wait_ge(setup_dve, 2)
                nc.vector.tensor_scalar(bias0[:], bg0[:], deg_col[:, 0:1], None, ALU.mult).then_inc(setup_dve, 1)
                dve.wait_ge(degree_mm, 1)
                nc.vector.tensor_scalar(bias1[:], psum[:, 7, 0:D], bg1[:, 0:1], None, ALU.mult).then_inc(bias1_ready, 1)
                dve.wait_ge(setup_dve, 3)
                dve.wait_ge(bias1_ready, 1)
                nc.vector.tensor_copy(wqk_parts[:, 0, :], wq[:, 0:2 * D]).then_inc(wqk_hi_done, 1)
                dve.wait_ge(wqk_hi_done, 1)
                nc.vector.tensor_tensor(wqk_parts[:, 1, :], wq[:, 0:2 * D], wqk_parts[:, 0, :].bitcast(F32),
                                        ALU.subtract).then_inc(wqk_split, 1)

                def max_of(it, j, b):
                    n = (it - 1) * GB + b
                    dve.wait_ge(score_mm, n + 1)
                    nc.vector.tensor_reduce(mx[:, b % 2, :], psum[:, 3 + b % 2, :].rearrange("p (h k) -> p h k", h=HEADS),
                                            AX.X, ALU.max).then_inc(max_ready, 1)

                def shift(it, j, b):
                    n = (it - 1) * GB + b
                    dve.wait_ge(max_ready, n + 1)
                    need(dve, exp_ready, n - 1)
                    nc.vector.tensor_tensor(sc[:, b % 2, :].rearrange("p (h k) -> p h k", h=HEADS),
                                            psum[:, 3 + b % 2, :].rearrange("p (h k) -> p h k", h=HEADS),
                                            mx[:, b % 2, :].unsqueeze(2).to_broadcast([D, HEADS, D]),
                                            ALU.subtract).then_inc(shifted, 1)

                def sums(it, j, b):
                    n = (it - 1) * GB + b
                    dve.wait_ge(exp_ready, n + 1)
                    nc.vector.tensor_reduce(den[:, (j + 3) % 4, b * HEADS:(b + 1) * HEADS],
                                            pr[:, (j + 1) % 2, b, :].rearrange("p (h k) -> p h k", h=HEADS),
                                            AX.X, ALU.add).then_inc(den_ready, 1)

                def add_h2_bias(it, j):
                    dve.wait_ge(h2_mm, it - 3)
                    need(dve, h2_ready, it - 5)
                    nc.vector.tensor_tensor(h2a[:, j % 2, :].rearrange("p (b t) -> p b t", b=GB),
                                            psum[:, 2, :].rearrange("p (b t) -> p b t", b=GB),
                                            bias1[:].unsqueeze(1).to_broadcast([D, GB, D]),
                                            ALU.add).then_inc(h2_added, 1)

                def inverse_sums(it, j):
                    dve.wait_ge(den_ready, (it - 2) * GB)
                    nc.vector.reciprocal(rden[:], den[:, (j + 1) % 4, :]).then_inc(rden_ready, 1)

                def scaled_attention(it, j):
                    g3 = it - 3
                    dve.wait_ge(rden_ready, g3 + 1)
                    dve.wait_ge(ot_rows, g3 + 1)
                    need(dve, res_ready, g3 - 1)
                    nc.vector.tensor_tensor(att[:, (j + 1) % 2, :].rearrange("p (a d) -> p a d", d=HD),
                                            psum[:, 0, :].rearrange("p (a d) -> p a d", d=HD),
                                            rden[:].unsqueeze(2).to_broadcast([D, GB * HEADS, HD]),
                                            ALU.mult).then_inc(att_ready, 1)

                def residual(it, j):
                    s3 = (j + 1) % 2
                    dve.wait_ge(att_ready, it - 2)
                    dve.wait_ge(xr_in[s3], slot_dmas(it, j, 3) + 16)
                    dve.wait_ge(x1_ready, it - 4)
                    nc.vector.tensor_tensor(res[:, s3, :], att[:, s3, :], xr[:, s3, :], ALU.add).then_inc(res_ready, 1)

                def statistics(it, j):
                    dve.wait_ge(res_ready, it - 2)
                    for b in range(GB):
                        ins = nc.vector.bn_stats(st6[:, b, :], res[:, (j + 1) % 2, b * D:(b + 1) * D])
                    ins.then_inc(stats_ready, 1)

                def moments(it, j):
                    dve.wait_ge(stats_ready, it - 2)
                    nc.vector.tensor_copy(tick[:, 1:2], tick[:, 0:1])
                    for b in range(GB):
                        ins = nc.vector.bn_aggr(mv[:, (j + 1) % 2, b, :], st6[:, b, :])
                    ins.then_inc(moments_ready, 1)

                def body(it, j):
                    if isinstance(it, int) and it == groups + 3:
                        step_cell(dve, 1, 0, 0)
                        add_h2_bias(it, j)
                        step_h(dve, 1, 0, 0)
                        return
                    g3 = it - 3
                    if isinstance(it, int) and it == groups + 2:
                        step_cell(dve, 0, 0, 0)
                    if norms(it):
                        inverse_sums(it, j)
                    if holds(it, 0):
                        dve.wait_ge(v_mm, it + 1)
                        need(dve, pv_mm, (it - 3) * GB)
                        nc.vector.tensor_copy(v_sb[:, j % 4, :], psum[:, 2, :]).then_inc(v_ready, 1)
                    if norms(it):
                        scaled_attention(it, j)
                        if last_with_pv(it):
                            residual(it, j)
                    if holds(it, 1):
                        max_of(it, j, 0)
                        shift(it, j, 0)
                    if norms(it):
                        statistics(it, j)
                        moments(it, j)
                    if holds(it, 1):
                        max_of(it, j, 1)
                        shift(it, j, 1)
                        sums(it, j, 0)
                        max_of(it, j, 2)
                        sums(it, j, 1)
                        shift(it, j, 2)
                    if holds(it, 4) and norms(it):
                        add_h2_bias(it, j)
                    if last_with_pv(it):
                        inverse_sums(it + 1, j + 1)
                        scaled_attention(it + 1, j + 1)
                        residual(it + 1, j + 1)
                        statistics(it + 1, j + 1)
                        moments(it + 1, j + 1)
                    if holds(it, 1):
                        max_of(it, j, 3)
                        sums(it, j, 2)
                        shift(it, j, 3)
                    if holds(it, 3):
                        dve.wait_ge(h1_mm, g3 + 1)
                        need(dve, h1_ready, g3 - 1)
                        nc.vector.tensor_tensor(h1a[:, (j + 1) % 2, :].rearrange("p (b t) -> p b t", b=GB),
                                                psum[:, 1, :].rearrange("p (b t) -> p b t", b=GB),
                                                bias0[:].unsqueeze(1).to_broadcast([D, GB, D]),
                                                ALU.add).then_inc(h1_added, 1)
                    if holds(it, 4) and not norms(it):
                        add_h2_bias(it, j)
                    if isinstance(it, int) and it == groups + 2:
                        step_h(dve, 0, 0, 0)
                    if holds(it, 1):
                        sums(it, j, 3)

                iterations(dve, body)

            def phase1_gpsimd(pool):
                for k_slot in k_sb:
                    nc.gpsimd.memset(k_slot[:], 0.0).then_inc(k_zeroed, 1)
                nc.gpsimd.memset(minus_half[:], -0.5).then_inc(half_set, 1)
                nc.gpsimd.memset(eps[:], EPS).then_inc(half_set, 1)
                nc.gpsimd.memset(zero[:], 0.0).then_inc(half_set, 1)
                pool.wait_ge(half_set, 3)
                for n in range(6):
                    p, part = n // 2, n % 2
                    pool.wait_ge(w_in[n % 2], 16 * (n // 2 + 1))
                    nc.gpsimd.tensor_copy(w_hi[:, p, part, :], w_raw[:, n % 2, :]).then_inc(w_hi_done, 1)
                    pool.wait_ge(w_hi_done, n + 1)
                    nc.gpsimd.tensor_tensor(w_lo[:, p, part, :], w_raw[:, n % 2, :],
                                            w_hi[:, p, part, :].bitcast(F32), ALU.subtract).then_inc(w_split, 1)

                def norm(it, j):
                    g3 = it - 3
                    s3 = (j + 1) % 2
                    if not isinstance(it, int) or it <= groups:
                        pool.wait_ge(att_ready, g3 + 1)
                        pool.wait_ge(xr_in[s3], slot_dmas(it, j, 3) + 16)
                        need(pool, x1_ready, g3 - 1)
                        nc.gpsimd.tensor_tensor(res[:, s3, :], att[:, s3, :], xr[:, s3, :], ALU.add).then_inc(res_ready, 1)
                    pool.wait_ge(moments_ready, g3 + 1)
                    nc.gpsimd.tensor_tensor(veps[:, s3, :], mv[:, s3, :, 1], eps[:, 0:GB], ALU.add).then_inc(veps_ready, 1)
                    if isinstance(it, int) and it > groups:
                        pool.wait_ge(shift_ready, g3)
                    nc.gpsimd.tensor_tensor(neg_mean[:], zero[:, 0:GB], mv[:, s3, :, 0], ALU.subtract).then_inc(neg_ready, 1)
                    pool.wait_ge(veps_ready, g3 + 1)
                    need(pool, x1_ready, g3 - 1)
                    nc.gpsimd.tensor_tensor(rstd[:, s3, :], veps[:, s3, :], minus_half[:, 0:GB], ALU.pow).then_inc(rstd_ready, 1)
                    pool.wait_ge(neg_ready, g3 + 1)
                    pool.wait_ge(rstd_ready, g3 + 1)
                    nc.gpsimd.tensor_tensor(nmr[:, s3, :], neg_mean[:], rstd[:, s3, :], ALU.mult).then_inc(shift_ready, 1)

                def split_x(it, j):
                    g = it + 1
                    pool.wait_ge(xt_in[(j + 1) % 2], slot_dmas(it, j, -1) + 16)
                    pool.wait_ge(k_mm, g)
                    nc.gpsimd.tensor_tensor(x_parts[:, 0, :].rearrange("p (b t) -> p b t", b=GB),
                                            xt[:, (j + 1) % 2, :].rearrange("p (b t) -> p b t", b=GB),
                                            ones[:].unsqueeze(1).to_broadcast([D, GB, D]), ALU.mult).then_inc(x_hi_done, 1)
                    pool.wait_ge(x_hi_done, g - (FIRST_SPLIT - 1))
                    nc.gpsimd.tensor_tensor(x_parts[:, 1, :], xt[:, (j + 1) % 2, :], x_parts[:, 0, :].bitcast(F32),
                                            ALU.subtract).then_inc(x_split, 1)

                def body(it, j):
                    if norms(it):
                        norm(it, j)
                    if not isinstance(it, int) or FIRST_SPLIT <= it + 1 < groups:
                        split_x(it, j)
                    if last_with_pv(it):
                        norm(it + 1, j + 1)

                pool.wait_ge(ones_ready, 1)
                iterations(pool, body)

        with ExitStack() as ctx:
            def s2(name, shape, dt=F32):
                return [sb(f"{name}{c}", shape, dt, ctx) for c in range(2)]

            h_all = s2("h_all", [D, UB, D])
            h_split = s2("h_split", [D, 2, UB, D], F32R)
            cell = s2("cell", [D, GW])
            tanh_c = s2("tanh_c", [D, GW])
            h_step = s2("h_step", [D, GW])
            h_step_split = s2("h_step_split", [D, 2, GW], F32R)
            ig = s2("ig", [D, GW])
            fc = s2("fc", [D, GW])
            res2 = s2("res2", [D, 2, GW])
            unit_stats = s2("unit_st6", [D, 2 * GB, 6])
            unit_moments = s2("unit_mv", [D, 2 * GB, 2])
            unit_veps = s2("unit_veps", [D, 2 * GB])
            unit_rstd = s2("unit_rstd", [D, 2 * GB])
            unit_neg_mean = s2("unit_neg_mean", [D, 2 * GB])
            unit_nmr = s2("unit_nmr", [D, 2 * GB])
            out_sb = s2("out_sb", [D, 2, GW])

            last_out_ready = sem("last_out_ready")
            scaled2_ready = sems2("scaled2_ready")
            prod_ready, cell_ready, tanh_ready, h_ready, hi_ready, split_ready = (
                sems2("prod_ready"), sems2("cell_ready"), sems2("tanh_ready"), sems2("h_ready"),
                sems2("hi_ready"), sems2("split_ready"))
            veps2_ready, neg2_ready, shift2_ready = sems2("veps2_ready"), sems2("neg2_ready"), sems2("shift2_ready")
            rows_mm, res2_ready, stats2_ready, moments2_ready, rstd2_ready, out_ready, out_sent = (
                sems2("rows_mm"), sems2("res2_ready"), sems2("stats2_ready"), sems2("moments2_ready"),
                sems2("rstd2_ready"), sems2("out_ready"), sems2("out_sent"))

            n_slots = len(slots)
            gates_before = [sum(len(slot_gates(s)) for _, s, _ in slots[:k]) for k in range(n_slots + 1)]
            n_gates = gates_before[-1]
            splits = n_slots - 1
            prods_before = [sum(2 for _, s, _ in slots[:k] if s > 0) for k in range(n_slots + 1)]
            n_prods = prods_before[-1]

            def gate_user(k, gate):
                for kk in range(k - 1, -1, -1):
                    if gate in slot_gates(slots[kk][1]):
                        return gates_before[kk] + slot_gates(slots[kk][1]).index(gate) + 1
                return None

            def width(slot):
                p, _, half = slot
                return GW if half is not None else UB * (D // p)

            def in_windows(ap, p, s):
                return ap[..., s:D // p * p:p] if D % p else ap[..., s::p]

            def shaped(ap, slot):
                p, _, half = slot
                b = UB // 2 if half is not None else UB
                return ap[:, 0:width(slot)].rearrange("p (b w) -> p b w", b=b)

            def h_view(ap, slot):
                p, s, half = slot
                if half is not None:
                    return ap[:, half * UB // 2:(half + 1) * UB // 2, :]
                return ap[:, :, s:D // p * p - p + s + 1:p]

            def step_gate(act, c, i, k, m):
                p, s, _ = slots[k]
                gate = slot_gates(s)[m]
                n = width(slots[k])
                if k > 0 and m == 0:
                    act.wait_ge(cell_ready[c], i * n_slots + k)
                if k > 0 and gate == GATE_O:
                    act.wait_ge(h_ready[c], i * n_slots + k)
                act.wait_ge(gate_mm[c], i * n_gates + (gates_before[k] + m + 1))
                nc.scalar.activation(gates[c][:, gate, 0:n], psum[:, BANK[c][gate], 0:n],
                                     ACT.Tanh if gate == GATE_G else ACT.Sigmoid,
                                     bias=b_lstm[:, p - 1, gate:gate + 1]).then_inc(gate_ready[c], 1)

            def step_tanh(act, c, i, k):
                n = width(slots[k])
                act.wait_ge(cell_ready[c], i * n_slots + (k + 1))
                nc.scalar.activation(tanh_c[c][:, 0:n], cell[c][:, 0:n], ACT.Tanh).then_inc(tanh_ready[c], 1)

            def step_cell(dve, c, i, k):
                n = width(slots[k])
                g_in = gates[c][:, :, 0:n]
                dve.wait_ge(gate_ready[c], i * n_gates + (gates_before[k] + 2))
                if slots[k][1] == 0:
                    nc.vector.tensor_tensor(cell[c][:, 0:n], g_in[:, GATE_I], g_in[:, GATE_G],
                                            ALU.mult).then_inc(cell_ready[c], 1)
                else:
                    nc.vector.tensor_tensor(ig[c][:, 0:n], g_in[:, GATE_I], g_in[:, GATE_G],
                                            ALU.mult).then_inc(prod_ready[c], 1)
                    dve.wait_ge(gate_ready[c], i * n_gates + (gates_before[k] + 3))
                    nc.vector.tensor_tensor(fc[c][:, 0:n], g_in[:, GATE_F], cell[c][:, 0:n],
                                            ALU.mult).then_inc(prod_ready[c], 1)
                    dve.wait_ge(prod_ready[c], i * n_prods + prods_before[k + 1])
                    nc.vector.tensor_tensor(cell[c][:, 0:n], ig[c][:, 0:n], fc[c][:, 0:n],
                                            ALU.add).then_inc(cell_ready[c], 1)

            def places_of_h(c, k):
                slot = slots[k]
                if slot[1] == slot[0] - 1:
                    return [slot, h_view(h_all[c], slot)] + [h_view(h_split[c][:, x], slot) for x in range(2)]
                return [slot, shaped(h_step[c], slot)] + [shaped(h_step_split[c][:, x], slot) for x in range(2)]

            def step_h(dve, c, i, k):
                slot, h32, hi, _ = places_of_h(c, k)
                dve.wait_ge(tanh_ready[c], i * n_slots + (k + 1))
                dve.wait_ge(gate_ready[c], i * n_gates + gates_before[k + 1])
                nc.vector.tensor_tensor(h32, shaped(gates[c][:, GATE_O], slot), shaped(tanh_c[c], slot),
                                        ALU.mult).then_inc(h_ready[c], 1)
                if k < n_slots - 1:
                    dve.wait_ge(h_ready[c], i * n_slots + (k + 1))
                    nc.vector.tensor_copy(hi, h32).then_inc(hi_ready[c], 1)

            def step_lo(dve, c, i, k):
                if 0 < k < n_slots - 1:
                    _, h32, hi, lo = places_of_h(c, k)
                    dve.wait_ge(hi_ready[c], i * splits + (k + 1))
                    if k == 1:
                        dve.wait_ge(split_ready[c], i * splits + 1)
                    nc.vector.tensor_tensor(lo, h32, hi.bitcast(F32), ALU.subtract).then_inc(split_ready[c], 1)

            n_pairs = units // 2
            EARLY = 4
            LATE_LO = (4, 5, 7, 8)

            def pairs(eng, body, tail):
                body(0, False)
                with eng.Fori(1, n_pairs) as i:
                    body(i, True)
                tail(n_pairs)

            def pair_cols(i, c, half):
                return bass.ds(i * (2 * UW) + (c * UW + half * GW), GW)

            def phase2_tensor(pe):
                def products(c, i, k, with_previous, part):
                    slot = slots[k]
                    p, s, half = slot
                    n = width(slot)
                    order = slot_gates(s)
                    if k == 0 and with_previous:
                        pe.wait_ge(gate_ready[c], i * n_gates)

                    hoisted = c == 0 and s == 1 and k > EARLY

                    def bank_free(gate):
                        last = gate_user(k, gate)
                        if last is not None:
                            pe.wait_ge(gate_ready[c], i * n_gates + last)
                        elif gate == GATE_F and with_previous:
                            pe.wait_ge(res2_ready[c], i * 2)

                    def product(gate, source, w_part, x_part, batches=slice(None), **flags):
                        bank = psum[:, BANK[c][gate], 0:n]
                        weights = (w_hi, w_lo)[w_part][:, p - 2, source, gate * D:(gate + 1) * D]
                        if source == 0:
                            return nc.tensor.matmul(shaped(bank, slot)[:, batches], weights,
                                                    h_view(h_split[c][:, x_part], slot)[:, batches], **flags)
                        return nc.tensor.matmul(bank, weights, h_step_split[c][:, x_part, 0:n], **flags)

                    def input_products(gate):
                        bank_free(gate)
                        product(gate, 0, 0, 0, start=True, stop=False)
                        product(gate, 0, 1, 0, start=False, stop=False)
                        product(gate, 0, 0, 1, start=False, stop=False)

                    if part == "inputs":
                        for gate in ((GATE_F,) if hoisted else ()) + (GATE_I, GATE_G, GATE_O):
                            input_products(gate)
                        return
                    if p == 1:
                        for gate in order:
                            bank_free(gate)
                            nc.tensor.matmul(psum[:, BANK[c][gate], 0:n], w_in1[:, gate * D:(gate + 1) * D],
                                             h2_cols[:, pair_cols(i, c, half)], start=True, stop=True).then_inc(gate_mm[c], 1)
                        return
                    if k == 2:
                        pe.wait_ge(split_ready[c], i * splits + 1)
                        for first in (True, False):
                            batches = slice(0, UB // 2) if first else slice(UB // 2, UB)
                            if not first:
                                pe.wait_ge(hi_ready[c], i * splits + 2)
                            for gate in order:
                                if first:
                                    bank_free(gate)
                                for w_part in range(2):
                                    product(gate, 0, w_part, 0, batches, start=(w_part == 0), stop=False)
                            if not first:
                                pe.wait_ge(split_ready[c], i * splits + 2)
                            for gate in order:
                                mm = product(gate, 0, 0, 1, batches, start=False, stop=True)
                                if not first:
                                    mm.then_inc(gate_mm[c], 1)
                        return
                    source, opens = (1, False) if s > 0 else (0, True)
                    pe.wait_ge(hi_ready[c], i * splits + k)
                    for gate in order[:2]:
                        if opens:
                            bank_free(gate)
                        product(gate, source, 0, 0, start=opens, stop=False)
                        product(gate, source, 1, 0, start=False, stop=False)
                    if s > 0 and not hoisted:
                        input_products(GATE_F)
                    pe.wait_ge(split_ready[c], i * splits + k)
                    for gate in order[:2]:
                        product(gate, source, 0, 1, start=False, stop=True).then_inc(gate_mm[c], 1)
                    for gate in order[2:]:
                        if opens:
                            bank_free(gate)
                        product(gate, source, 0, 0, start=opens, stop=False)
                        product(gate, source, 1, 0, start=False, stop=False)
                        product(gate, source, 0, 1, start=False, stop=True).then_inc(gate_mm[c], 1)

                def rows(c, i, half, bank):
                    if half == 0:
                        pe.wait_ge(h_ready[c], i * n_slots)
                        pe.wait_ge(gate_ready[c], i * n_gates)
                    elif bank == GATE_F:
                        pe.wait_ge(res2_ready[c], i * 2 - 1)
                    for b in range(GB):
                        mm = nc.tensor.transpose(psum[:, BANK[c][bank], b * D:(b + 1) * D],
                                                 h_all[c][:, half * GB + b, :], ident[:])
                    mm.then_inc(rows_mm[c], 1)

                def body(i, with_previous):
                    for k in range(n_slots):
                        for c in range(2):
                            if slots[k][1] > 0 and not (c == 0 and slots[k][1] == 1 and k > EARLY):
                                products(c, i, k, with_previous, "inputs")
                            if with_previous or (k > 0 and (k, c) != (1, 0)):
                                products(c, i, k, with_previous, "rest")
                            if c == 0 and k >= EARLY and slots[k][1] == 0:
                                products(0, i, k + 1, with_previous, "inputs")
                            if with_previous and k < 2:
                                rows(c, i, k, GATE_F)

                def tail(i):
                    for c in range(2):
                        rows(c, i, 0, GATE_F)
                        rows(c, i, 1, GATE_I)

                pairs(pe, body, tail)

            def phase2_scalar(act):
                def normalized(c, batches):
                    for b in batches:
                        at = slice(b % GB * D, (b % GB + 1) * D)
                        ins = nc.scalar.activation(out_sb[c][:, b // GB, at], res2[c][:, b // GB, at], ACT.Identity,
                                                   bias=unit_nmr[c][:, b:b + 1], scale=unit_rstd[c][:, b:b + 1])
                    return ins

                def body(i, with_previous):
                    for k, slot in enumerate(slots):
                        if k == 2 and not with_previous:
                            phase1_over(act)
                        for c in range(2):
                            if not with_previous and k == 0:
                                continue
                            for m in range(len(slot_gates(slot[1]))):
                                step_gate(act, c, i, k, m)
                            step_tanh(act, c, i, k)

                def tail(i):
                    for c in range(2):
                        act.wait_ge(out_sent[c], 16 * (n_pairs - 1))
                        for half in range(2):
                            act.wait_ge(shift2_ready[c], i + half)
                            last = (c, half) == (1, 1)
                            normalized(c, range(half * GB, half * GB + (2 if last else GB))).then_inc(out_ready[c], 1)

                pairs(act, body, tail)

            def phase2_vector(dve):
                def residual(c, i, half, bank):
                    dve.wait_ge(rows_mm[c], i * 2 - 1 + half)
                    nc.vector.tensor_tensor(res2[c][:, half, :], psum[:, BANK[c][bank], :],
                                            x1_rows[:, pair_cols(i - 1, c, half)], ALU.add).then_inc(res2_ready[c], 1)

                def statistics(c, i, half):
                    dve.wait_ge(res2_ready[c], i * 2 - 1 + half)
                    for b in range(half * GB, (half + 1) * GB):
                        ins = nc.vector.bn_stats(unit_stats[c][:, b, :], res2[c][:, half, b % GB * D:(b % GB + 1) * D])
                    ins.then_inc(stats2_ready[c], 1)

                def moments(c, n_stats, batches):
                    dve.wait_ge(stats2_ready[c], n_stats)
                    nc.vector.tensor_copy(tick[:, 1:2], tick[:, 0:1])
                    for b in batches:
                        ins = nc.vector.bn_aggr(unit_moments[c][:, b, :], unit_stats[c][:, b, :])
                    ins.then_inc(moments2_ready[c], 1)

                def body(i, with_previous):
                    for k in range(n_slots):
                        if k == 2 and not with_previous:
                            phase1_over(dve)
                        for c in range(2):
                            if not with_previous and k == 0:
                                continue
                            step_cell(dve, c, i, k)
                            if c == 0 and k in LATE_LO:
                                step_lo(dve, 1, i, k - 1)
                            if with_previous:
                                if k < 2:
                                    residual(c, i, k, GATE_F)
                                elif k < 4:
                                    statistics(c, i, k - 2)
                                elif k == 4:
                                    moments(c, i * 2, range(UB))
                            step_h(dve, c, i, k)
                            if not (c == 1 and k + 1 in LATE_LO):
                                step_lo(dve, c, i, k)
                    if with_previous:
                        for c in range(2):
                            dve.wait_ge(out_ready[c], i)

                def tail(i):
                    halves = [(c, half) for c in range(2) for half in range(2)]
                    for n in range(len(halves) + 2):
                        if n < len(halves):
                            c, half = halves[n]
                            residual(c, i, half, (GATE_F, GATE_I)[half])
                        if n > 1:
                            c, half = halves[n - 2]
                            moments(c, i * 2 - 1 + half, range(half * GB, (half + 1) * GB))
                        if 1 <= n <= len(halves):
                            last_c, last_half = halves[n - 1]
                            statistics(last_c, i, last_half)
                    dve.wait_ge(out_sent[1], 16 * (n_pairs - 1))
                    dve.wait_ge(shift2_ready[1], i + 1)
                    for b in (UB - 2, UB - 1):
                        at = slice(b % GB * D, (b % GB + 1) * D)
                        ins = nc.vector.tensor_scalar(out_sb[1][:, 1, at], res2[1][:, 1, at], unit_rstd[1][:, b:b + 1],
                                                      unit_nmr[1][:, b:b + 1], ALU.mult, ALU.add)
                    ins.then_inc(last_out_ready, 1)

                pairs(dve, body, tail)

            def phase2_gpsimd(pool):
                def scales(c, at, n):
                    pool.wait_ge(moments2_ready[c], n)
                    nc.gpsimd.tensor_tensor(unit_veps[c][:, at], unit_moments[c][:, at, 1], eps[:, at], ALU.add).then_inc(veps2_ready[c], 1)
                    nc.gpsimd.tensor_tensor(unit_neg_mean[c][:, at], zero[:, at], unit_moments[c][:, at, 0],
                                            ALU.subtract).then_inc(neg2_ready[c], 1)
                    pool.wait_ge(veps2_ready[c], n)
                    nc.gpsimd.tensor_tensor(unit_rstd[c][:, at], unit_veps[c][:, at], minus_half[:, at], ALU.pow).then_inc(rstd2_ready[c], 1)
                    pool.wait_ge(neg2_ready[c], n)
                    pool.wait_ge(rstd2_ready[c], n)
                    nc.gpsimd.tensor_tensor(unit_nmr[c][:, at], unit_neg_mean[c][:, at], unit_rstd[c][:, at],
                                            ALU.mult).then_inc(shift2_ready[c], 1)

                def first_lo(c, i):
                    hi, lo = (h_view(h_split[c][:, x], slots[0]) for x in range(2))
                    pool.wait_ge(hi_ready[c], i * splits + 1)
                    nc.gpsimd.tensor_tensor(lo, h_view(h_all[c], slots[0]), hi.bitcast(F32),
                                            ALU.subtract).then_inc(split_ready[c], 1)

                for c in range(2):
                    first_lo(c, 0)
                with pool.Fori(1, n_pairs) as i:
                    for c in range(2):
                        first_lo(c, i)
                    for c in range(2):
                        scales(c, slice(0, UB), i)
                    for c in range(2):
                        scale, add = (v[c][:].unsqueeze(2).to_broadcast([D, UB, D]) for v in (unit_rstd, unit_nmr))
                        unit = out_sb[c][:].rearrange("p a (b d) -> p (a b) d", d=D)
                        nc.gpsimd.tensor_tensor(unit, res2[c][:].rearrange("p a (b d) -> p (a b) d", d=D), scale,
                                                ALU.mult).then_inc(scaled2_ready[c], 1)
                        pool.wait_ge(shift2_ready[c], i)
                        pool.wait_ge(scaled2_ready[c], i)
                        nc.gpsimd.tensor_tensor(unit, unit, add, ALU.add).then_inc(out_ready[c], 1)
                    for c in range(2):
                        pool.wait_ge(out_sent[c], i * 16)
                for c in range(2):
                    for half in range(2):
                        scales(c, slice(half * GB, (half + 1) * GB), n_pairs + half)

            def phase2_sync(sp):
                with sp.Fori(0, n_pairs - 1) as i:
                    for c in range(2):
                        at = sp.snap(i * (2 * UW) + c * UW)
                        sp.wait_ge(out_ready[c], i + 1)
                        sp.dma_start(out[:, bass.ds(at, UW)],
                                     out_sb[c][:].rearrange("p a b -> p (a b)")).then_inc(out_sent[c], 16)
                for c in range(2):
                    for half in range(2):
                        sp.wait_ge(out_ready[c], n_pairs + half)
                        if (c, half) == (1, 1):
                            sp.wait_ge(last_out_ready, 1)
                        sp.dma_start(out[:, pair_cols(n_pairs - 1, c, half)], out_sb[c][:, half]).then_inc(out_sent[c], 16)
                for c in range(2):
                    sp.wait_ge(out_sent[c], 16 * (n_pairs + 1))

        def phase1_over(eng):
            eng.wait_ge(h2_ready, groups)
            for kept in x1_kept:
                eng.wait_ge(kept, 16 * (groups // 2))

        with nc.Block() as block:
            @block.sync
            def _(sp):
                phase1_sync(sp)
                phase2_sync(sp)

            @block.tensor
            def _(pe):
                phase1_tensor(pe)
                phase2_tensor(pe)

            @block.scalar
            def _(act):
                phase1_scalar(act)
                phase2_scalar(act)

            @block.vector
            def _(dve):
                phase1_vector(dve)
                phase2_vector(dve)

            @block.gpsimd
            def _(pool):
                phase1_gpsimd(pool)
                phase2_gpsimd(pool)


def kernel(x, adj, L0_gnn_W, L1_gnn_Wg0, L1_gnn_bg0, L1_gnn_Wg1, L1_gnn_bg1,
           L1_gnn_Wih, L1_gnn_Whh, L1_gnn_bih, L1_gnn_bhh):
    import numpy as np
    import concourse.bacc as bacc
    from concourse.bass_utils import run_bass_kernel_spmd

    x, adj = np.asarray(x), np.asarray(adj)
    batches, nodes, feats = x.shape
    arrays = {
        "x_cols": x.transpose(2, 0, 1).reshape(feats, batches * nodes),
        "x_rows": x.transpose(1, 0, 2).reshape(nodes, batches * feats),
        "adj": adj,
        "adj_t": adj.T,
        "w_qkv": np.asarray(L0_gnn_W),
        "w_g0": np.asarray(L1_gnn_Wg0),
        "b_g0": np.broadcast_to(np.asarray(L1_gnn_bg0)[None, :], (nodes, feats)),
        "w_g1": np.asarray(L1_gnn_Wg1),
        "b_g1": np.asarray(L1_gnn_bg1)[:, None],
        "w_ih": np.asarray(L1_gnn_Wih).transpose(2, 0, 1),
        "w_hh": np.asarray(L1_gnn_Whh).transpose(2, 0, 1),
        "b_ih": np.asarray(L1_gnn_bih).reshape(-1, 4, feats).transpose(2, 0, 1),
        "b_hh": np.asarray(L1_gnn_bhh).reshape(-1, 4, feats).transpose(2, 0, 1),
        "eye": np.eye(feats, dtype=np.float32),
    }
    arrays = {name: np.ascontiguousarray(a) for name, a in arrays.items()}
    nc = bacc.Bacc("TRN2", target_bir_lowering=False, num_devices=1)
    args = [nc.dram_tensor(name, a.shape, mybir.dt.from_np(a.dtype), kind="ExternalInput").ap()
            for name, a in arrays.items()]
    out = nc.dram_tensor("out", (nodes, batches * feats), F32, kind="ExternalOutput").ap()
    adjacent_residual_kernel(nc, *args, out)
    result = run_bass_kernel_spmd(nc, [arrays], core_ids=[0])
    rows = result.results[0]["out"]
    return rows.reshape(nodes, batches, feats).transpose(1, 0, 2)
```
